# Optimizing a Trainium2 kernel written in Bass

```python
import numpy as np
import jax
import jax.numpy as jnp

def _softmax(x, axis=-1):
    return jax.nn.softmax(x, axis=axis)

def _gelu(x):
    return jax.nn.gelu(x, approximate=True)

def _silu(x):
    return jax.nn.silu(x)

def _sigmoid(x):
    return jax.nn.sigmoid(x)

def _layernorm(x, axis=-1, eps=1e-05):
    m = jnp.mean(x, axis=axis, keepdims=True)
    v = jnp.var(x, axis=axis, keepdims=True)
    return (x - m) / jnp.sqrt(v + eps)

def _scatter_add(tgt, idx, src, axis=0):
    return tgt.at[idx].add(src)

def _segment_sum(src, seg, n):
    return jax.ops.segment_sum(src, seg, n)
kernel_name = 'mk_vit_tower_d1_tok_img1024_r4_437778'

def setup_inputs(seed: int=0):
    np.random.seed(seed)
    _w = jnp.asarray

    def _rec_inputs():
        import jax
        import jax.numpy as jnp
        _rk = jax.random.key(seed)
        x = -0.00150118 + 0.499729 * jax.random.normal(jax.random.fold_in(_rk, 1), (16, 256, 64, 2), jnp.float32)
        return x
    x = _rec_inputs()

    def _L0_tok_setup():
        import jax, jax.numpy as jnp
        import numpy as np
        import math
        H = 256
        N = 64
        CH = 1
        SEQ_L = 256
        key = jax.random.key(seed)
        k1, k2, k3, k4 = jax.random.split(key, 4)
        log_dt = jax.random.uniform(k1, (H,), dtype=jnp.float32, minval=math.log(0.001), maxval=math.log(0.1))
        inv_A_real = jnp.log(0.5 * jnp.ones((H, N), jnp.float32)) + 0.1 * jax.random.normal(k2, (H, N), dtype=jnp.float32)
        A_imag = jnp.broadcast_to(math.pi * jnp.arange(N, dtype=jnp.float32), (H, N)).copy()
        B_ri = jax.random.normal(k3, (H, N, 2), dtype=jnp.float32) * 0.5
        C_ri = jax.random.normal(k4, (CH, H, N, 2), dtype=jnp.float32) * 0.5
        return {'log_dt': log_dt, 'inv_A_real': inv_A_real, 'A_imag': A_imag, 'B_ri': B_ri, 'C_ri': C_ri, 'L': SEQ_L}
    _L0_tok_all = _L0_tok_setup()
    _L0_tok_in = {k: v for k, v in _L0_tok_all.items() if k in ('log_dt', 'inv_A_real', 'A_imag', 'B_ri')}
    del _L0_tok_all

    def _L0_attn_setup():
        import jax, jax.numpy as jnp
        import numpy as np
        DIM, H, G = (256, 16, 4)
        HD = DIM // H
        HKV = H // G

        def rotate_half(x):
            return jnp.concatenate([-x[..., 1::2], x[..., ::2]], axis=-1)

        def rope_tables(seq_len, dim, dtype):
            inv_freq = 1.0 / 10000.0 ** (jnp.arange(0, dim, 2, dtype=jnp.float32) / dim)
            pos = jnp.arange(seq_len, dtype=jnp.float32)
            sinusoid = pos[:, None] * inv_freq[None, :]
            sin = jnp.concatenate([jnp.sin(sinusoid)] * 2, -1)
            cos = jnp.concatenate([jnp.cos(sinusoid)] * 2, -1)
            return (sin.astype(dtype)[None, :, None, :], cos.astype(dtype)[None, :, None, :])
        key = jax.random.key(seed)
        ks = jax.random.split(key, 9)
        s = 0.02
        return {'hidden_states': jax.random.normal(ks[0], (2, 512, DIM), jnp.float32), 'Wq': jax.random.normal(ks[1], (DIM, DIM), jnp.float32) * s, 'bq': jnp.zeros((DIM,), jnp.float32), 'Wk': jax.random.normal(ks[2], (DIM // G, DIM), jnp.float32) * s, 'bk': jnp.zeros((DIM // G,), jnp.float32), 'Wv': jax.random.normal(ks[3], (DIM // G, DIM), jnp.float32) * s, 'bv': jnp.zeros((DIM // G,), jnp.float32), 'Wo': jax.random.normal(ks[4], (DIM, DIM), jnp.float32) * s, 'bo': jnp.zeros((DIM,), jnp.float32)}
    _L0_attn_all = _L0_attn_setup()
    _L0_attn_in = {k: v for k, v in _L0_attn_all.items() if k in ('Wq', 'bq', 'Wk', 'bk', 'Wv', 'bv', 'Wo', 'bo')}
    del _L0_attn_all

    def _L0_ffn_setup():
        import jax, jax.numpy as jnp
        import numpy as np
        D_MODEL = 256
        EXPERT_DIM = 128
        N_EXPERTS = 8
        TOP_K = 2

        def _sq_relu(h):
            return jnp.square(jax.nn.relu(h))
        key = jax.random.key(seed)
        ks = jax.random.split(key, 6)
        s = 0.02
        x = jax.random.normal(ks[0], (2, 512, D_MODEL), dtype=jnp.float32)
        Ws1 = jax.random.normal(ks[1], (D_MODEL, EXPERT_DIM), dtype=jnp.float32) * s
        Ws2 = jax.random.normal(ks[2], (EXPERT_DIM, D_MODEL), dtype=jnp.float32) * s
        W1 = jax.random.normal(ks[3], (N_EXPERTS, D_MODEL, EXPERT_DIM), dtype=jnp.float32) * s
        W2 = jax.random.normal(ks[4], (N_EXPERTS, EXPERT_DIM, D_MODEL), dtype=jnp.float32) * s
        Wr = jax.random.normal(ks[5], (D_MODEL, N_EXPERTS), dtype=jnp.float32) * s
        return {'x': x, 'Ws1': Ws1, 'Ws2': Ws2, 'W1': W1, 'W2': W2, 'Wr': Wr}
    _L0_ffn_all = _L0_ffn_setup()
    _L0_ffn_in = {k: v for k, v in _L0_ffn_all.items() if k in ('Ws1', 'Ws2', 'W1', 'W2', 'Wr')}
    del _L0_ffn_all
    return {'x': x, 'L0_tok_log_dt': _L0_tok_in['log_dt'], 'L0_tok_inv_A_real': _L0_tok_in['inv_A_real'], 'L0_tok_A_imag': _L0_tok_in['A_imag'], 'L0_tok_B_ri': _L0_tok_in['B_ri'], 'L0_attn_Wq': _L0_attn_in['Wq'], 'L0_attn_bq': _L0_attn_in['bq'], 'L0_attn_Wk': _L0_attn_in['Wk'], 'L0_attn_bk': _L0_attn_in['bk'], 'L0_attn_Wv': _L0_attn_in['Wv'], 'L0_attn_bv': _L0_attn_in['bv'], 'L0_attn_Wo': _L0_attn_in['Wo'], 'L0_attn_bo': _L0_attn_in['bo'], 'L0_ffn_Ws1': _L0_ffn_in['Ws1'], 'L0_ffn_Ws2': _L0_ffn_in['Ws2'], 'L0_ffn_W1': _L0_ffn_in['W1'], 'L0_ffn_W2': _L0_ffn_in['W2'], 'L0_ffn_Wr': _L0_ffn_in['Wr']}

def reference(x, L0_tok_log_dt, L0_tok_inv_A_real, L0_tok_A_imag, L0_tok_B_ri, L0_attn_Wq, L0_attn_bq, L0_attn_Wk, L0_attn_bk, L0_attn_Wv, L0_attn_bv, L0_attn_Wo, L0_attn_bo, L0_ffn_Ws1, L0_ffn_Ws2, L0_ffn_W1, L0_ffn_W2, L0_ffn_Wr):
    import jax
    import jax.numpy as jnp

    def _L0_tok_ref(log_dt, inv_A_real, A_imag, B_ri, C_ri, L):
        import jax, jax.numpy as jnp
        import numpy as np
        import math
        H = 256
        N = 64
        CH = 1
        SEQ_L = 256
        dt = jnp.exp(log_dt)
        A = -jnp.exp(inv_A_real) + 1j * A_imag
        B = B_ri[..., 0] + 1j * B_ri[..., 1]
        C = C_ri[..., 0] + 1j * C_ri[..., 1]
        dtA = A * dt[:, None]
        dA = (1.0 + dtA / 2) / (1.0 - dtA / 2)
        C_term = C * B[None]
        log_dA = jnp.log(dA)
        V = jnp.exp(log_dA[:, :, None] * jnp.arange(L))
        K = 2.0 * jnp.einsum('chn,hnl->chl', C_term, V).real
        return K.astype(jnp.float32)

    def _L0_attn_ref(hidden_states, Wq, bq, Wk, bk, Wv, bv, Wo, bo):
        import jax, jax.numpy as jnp
        import numpy as np
        DIM, H, G = (256, 16, 4)
        HD = DIM // H
        HKV = H // G

        def rotate_half(x):
            return jnp.concatenate([-x[..., 1::2], x[..., ::2]], axis=-1)

        def rope_tables(seq_len, dim, dtype):
            inv_freq = 1.0 / 10000.0 ** (jnp.arange(0, dim, 2, dtype=jnp.float32) / dim)
            pos = jnp.arange(seq_len, dtype=jnp.float32)
            sinusoid = pos[:, None] * inv_freq[None, :]
            sin = jnp.concatenate([jnp.sin(sinusoid)] * 2, -1)
            cos = jnp.concatenate([jnp.cos(sinusoid)] * 2, -1)
            return (sin.astype(dtype)[None, :, None, :], cos.astype(dtype)[None, :, None, :])
        b, t, _ = hidden_states.shape
        q = (hidden_states @ Wq.T + bq).reshape(b, t, H, HD)
        k = (hidden_states @ Wk.T + bk).reshape(b, t, HKV, HD)
        v = (hidden_states @ Wv.T + bv).reshape(b, t, HKV, HD)
        sin, cos = rope_tables(t, HD, q.dtype)
        q = q * cos + rotate_half(q) * sin
        k = k * cos + rotate_half(k) * sin
        k = jnp.repeat(k, G, axis=2)
        v = jnp.repeat(v, G, axis=2)
        scale = 1.0 / jnp.sqrt(jnp.float32(HD)).astype(q.dtype)
        scores = jnp.einsum('bthd,bshd->btsh', q, k) * scale
        probs = jax.nn.softmax(scores, axis=2)
        context = jnp.einsum('btsh,bshd->bthd', probs, v).reshape(b, t, DIM)
        return context @ Wo.T + bo

    def _L0_ffn_ref(x, Ws1, Ws2, W1, W2, Wr):
        import jax, jax.numpy as jnp
        import numpy as np
        D_MODEL = 256
        EXPERT_DIM = 128
        N_EXPERTS = 8
        TOP_K = 2

        def _sq_relu(h):
            return jnp.square(jax.nn.relu(h))
        shape = x.shape
        xf = x.reshape(-1, D_MODEL)
        out_shared = _sq_relu(xf @ Ws1) @ Ws2
        logits = xf @ Wr
        top_vals, top_idx = jax.lax.top_k(logits, TOP_K)
        rw = jax.nn.softmax(top_vals.astype(jnp.float32), axis=-1).astype(x.dtype)
        onehot = jax.nn.one_hot(top_idx, N_EXPERTS, dtype=x.dtype)
        prob = jnp.einsum('tk,tke->te', rw, onehot)
        prob = jnp.trunc(prob)
        h = _sq_relu(jnp.einsum('td,edf->tef', xf, W1))
        y = jnp.einsum('tef,efd->ted', h, W2)
        out_routed = jnp.einsum('ted,te->td', y, prob)
        return (out_shared + out_routed).reshape(shape)
    h = _L0_tok_ref(L0_tok_log_dt, L0_tok_inv_A_real, L0_tok_A_imag, L0_tok_B_ri, x, 256)
    h = h + _L0_attn_ref(_layernorm(h, axis=-1), L0_attn_Wq, L0_attn_bq, L0_attn_Wk, L0_attn_bk, L0_attn_Wv, L0_attn_bv, L0_attn_Wo, L0_attn_bo)
    h = h + _L0_ffn_ref(_layernorm(h, axis=-1), L0_ffn_Ws1, L0_ffn_Ws2, L0_ffn_W1, L0_ffn_W2, L0_ffn_Wr)
    return h

_drawn_inputs = setup_inputs


def setup_inputs(seed=0):
    import zlib

    import numpy as np

    out = dict(_drawn_inputs(seed))
    spreads = {'L0_attn_bq': (0.0, 0.8),
     'L0_attn_bk': (0.0, 0.8),
     'L0_attn_bv': (0.0, 0.8),
     'L0_attn_bo': (0.0, 0.353)}
    factors = {'L0_attn_Wq': 8.0,
     'L0_attn_Wk': 8.0,
     'L0_attn_Wv': 8.0,
     'L0_attn_Wo': 7.267,
     'L0_ffn_Ws1': 8.0,
     'L0_ffn_Ws2': 8.0}
    for name, (base, spread) in spreads.items():
        noise = np.random.default_rng([zlib.crc32(name.encode()), seed]).standard_normal(out[name].shape)
        drawn = base * np.exp(spread * noise) if base else spread * noise
        out[name] = jnp.asarray(drawn.astype(out[name].dtype))
    for name, factor in factors.items():
        out[name] = (out[name] * factor).astype(out[name].dtype)
    return out
```

```python
from contextlib import ExitStack

import numpy as np

import concourse.bass as bass
from concourse import mybir

F32 = mybir.dt.float32
BF16 = mybir.dt.bfloat16
I32 = mybir.dt.int32
ACT = mybir.ActivationFunctionType
ALU = mybir.AluOpType
AX = mybir.AxisListType

P = 128
CH, SEQ, NS = 16, 256, 64
D = 256
TT = SEQ // P
A_N, B_N = 4, 64
NH, NKV, HD = 16, 4, 16
GQ = NH // NKV
QK_COLS = (NH + NKV) * HD
QKV = QK_COLS + NKV * HD
COL = 32
STACK = 6 * HD
KROWS = STACK + 3
UNITS = NH // 2
SCALE = 1.0 / float(np.sqrt(HD))
EPS = 1e-5
FF = 128
NE = 8
GH = 8
GROUPS = P // GH
GC = 2 * GH * B_N


class Batch:

    def __init__(self, base, half, shift):
        self.n = base + shift if isinstance(base, int) else base + shift
        self.static = isinstance(base, int)
        self.parity = shift % 2 if not self.static else self.n % 2
        self.half = half + shift // 2 if not self.static else self.n // 2
        self.back = lambda k: Batch(base, half, shift - k)

    @property
    def real(self):
        return not self.static or 0 <= self.n < CH

    def index(self):
        return slice(self.n, self.n + 1) if self.static else bass.ds(self.n, 1)


def steps(eng, step):
    for s in range(-3, 2):
        step(Batch(s, None, 0))
    with eng.Fori(1, CH // 2 - 2) as i:
        for par in range(2):
            step(Batch(2 * i, i, par))
    for s in range(CH - 4, CH + 1):
        step(Batch(s, None, 0))


def vit_block_kernel(nc, xh, log_dt, inv_a, a_imag, b_ri, wqkv, bqkv, wo, bo, ws1, ws2, w1, w2, wr,
                     cos_t, sin_t, ident_d, out):
    with ExitStack() as ctx:
        def sb(name, shape, dt=F32):
            return ctx.enter_context(nc.sbuf_tensor(name, shape, dt))

        def sem(name):
            return ctx.enter_context(nc.semaphore(name))

        h_feat = sb("h_feat", [P, CH, A_N, P])
        h_all = sb("h_all", [P, CH, TT, D])
        region = sb("region", [P, 8192])
        arena = sb("arena", [P, 12032])
        x2_keep = nc.dram_tensor("x2_keep", [CH, P, 2 * SEQ], F32, kind="Internal").ap()
        ident = sb("ident", [P, P])
        ident_b = sb("ident_b", [P, P], BF16)
        wqkv_sb = sb("wqkv_sb", [P, 2, QKV])
        wo_sb = sb("wo_sb", [P, 2, D])
        ws1_sb = sb("ws1_sb", [P, 2, FF])
        ws2_sb = sb("ws2_sb", [P, D])
        wr_sb = sb("wr_sb", [P, 2, NE])
        bqkv_sb = sb("bqkv_sb", [P, QKV])
        bo_sb = sb("bo_sb", [P, D])
        cos_sb = sb("cos_sb", [P, TT, HD])
        sin_sb = sb("sin_sb", [P, TT, HD])
        eps_pow = sb("eps_pow", [P, TT])
        carrier = sb("carrier", [P, 1])
        eps_tile = sb("eps_tile", [P, TT])
        h_slice = [sb(f"h_slice{i}", [P, A_N, P]) for i in range(2)]
        stats = [sb(f"stats{i}", [P, TT, 6]) for i in range(2)]
        mean_var = [sb(f"mean_var{i}", [P, TT, 2]) for i in range(2)]
        var_eps = [sb(f"var_eps{i}", [P, TT]) for i in range(2)]
        rstd = [sb(f"rstd{i}", [P, TT]) for i in range(2)]
        qkv = sb("qkv", [P, TT, QKV])
        rope_sum_sb = sb("rope_sum", [P, TT, QK_COLS])
        zeros = sb("zeros", [NH, SEQ])
        q_parts = sb("q_parts", [P, TT, NH, STACK], BF16)
        k_parts = sb("k_parts", [P, TT, NKV, KROWS], BF16)
        v_max = [sb(f"v_max{i}", [P, TT, NKV, COL]) for i in range(2)]
        v_exp = [sb(f"v_exp{i}", [P, TT, NKV, COL]) for i in range(2)]
        neg_max = sb("neg_max", [P, TT, NKV, GQ])
        neg_max_t = sb("neg_max_t", [NH, SEQ])
        max_rest = sb("max_rest", [NH, SEQ])
        max_parts = [sb(f"max_parts{i}", [NH, 3, SEQ], BF16) for i in range(2)]
        ctx_sum = sb("ctx_sum", [P, TT, GQ, NKV])
        ctx_n = sb("ctx_n", [P, TT, NKV, GQ, HD])
        hid_relu = sb("hid_relu", [FF, SEQ])
        hid = sb("hid", [FF, SEQ])
        logits = sb("logits", [P, CH, TT * NE])

        def family(m, at, src):
            return src[:, at:at + 512 * m].rearrange("p (m r h) -> p m r h", m=m, r=2)

        low = family(8, 0, arena)
        high = family(8, 4096, arena)
        gain = family(A_N, 8192, arena)
        par_sb = arena[:, 10240:11520].rearrange("p (k h) -> p k h", k=5)
        hall_flat = h_all[:].rearrange("p c t f -> p (c t f)")
        ca = hall_flat[:, 0:4096].rearrange("p (c h) -> p c h", c=CH)
        cb = hall_flat[:, 4096:8192].rearrange("p (c h) -> p c h", c=CH)
        prod = [[region[:, (4 * i + k) * GC:(4 * i + k + 1) * GC] for k in range(4)] for i in range(2)]
        hf_flat = h_feat[:].rearrange("p c a t -> p (c a t)")
        squares = family(5, 0, hf_flat)
        tmp_re, tmp_im, tmp_sq = family(4, 2560, hf_flat), family(4, 4608, hf_flat), family(1, 6656, hf_flat)
        small = region[:, 0:2304].rearrange("p (k h) -> p k h", k=9)
        q_max, q_exp = ([region[:, 2048 * (2 * k + i):2048 * (2 * k + i + 1)].bitcast(BF16)
                         .rearrange("p (n t) -> p n t", n=NH) for i in range(2)] for k in range(2))
        k_max, k_exp = ([arena[:, 512 * (2 * k + i):512 * (2 * k + i + 1)].bitcast(BF16)
                         .rearrange("p (j t) -> p j t", j=NKV) for i in range(2)] for k in range(2))
        probs = [arena[:, 2048 + 2048 * i:2048 + 2048 * (i + 1)].rearrange("p (j f) -> p j f", j=NKV)
                 for i in range(2)]

        xn, x_t, xn2, ctx_t, x2_t0, x2_t1 = (arena[:, o:o + 512].rearrange("p (k t) -> p k t", k=2)
                                             for o in range(6144, 9216, 512))
        x2_t = [x2_t0, x2_t1]
        ctx_raw = arena[:, 9216:10240].rearrange("p (g t) -> p g t", g=GQ)

        rope_c, rope_s, rope_sum = (arena[:, 10240 + k * 2 * QK_COLS:10240 + (k + 1) * 2 * QK_COLS]
                                    .rearrange("p (t f) -> p t f", t=TT)
                                    if k < 2 else rope_sum_sb[:] for k in range(3))

        w1_e = arena[:, 0:2 * FF].rearrange("p (k f) -> p k f", k=2)
        w2_e = arena[:, 256:256 + D]
        x2_e = arena[:, 512:1024].rearrange("p (k t) -> p k t", k=2)
        tiles = CH * TT
        route = arena[:, 1024:1024 + 12 * tiles]
        top1, top2, n_top, exp_gap, gate = (route[:, tiles * k:tiles * (k + 1)] for k in range(5))
        is_top = arena[:, 2048:2048 + tiles * NE].rearrange("p (t e) -> p t e", e=NE)
        others = arena[:, 2304:2304 + tiles * NE].rearrange("p (t e) -> p t e", e=NE)
        weight = arena[:, 2560:2560 + tiles * NE]
        any_gate = sb("any_gate", [P, 2])
        routed_n = sb("routed_n", [1, 1], I32)

        max_ps = ctx.enter_context(nc.psum_tensor("max_ps", [P, 2, 512], F32))
        exp_ps = ctx.enter_context(nc.psum_tensor("exp_ps", [P, 2, 512], F32))
        ctx_ps = [ctx.enter_context(nc.psum_tensor(f"ctx_ps{i}", [P, 512], F32)) for i in range(2)]
        misc = [ctx.enter_context(nc.psum_tensor(f"misc{i}", [P, 512], F32)) for i in range(2)]

        ld_dt, ld_par, ld_c, ld_w, ld_id = (sem(f"ld_{n}") for n in ("dt", "par", "c", "w", "id"))
        exp_par = sem("exp_par")
        firsts = sem("firsts")
        chain = sem("chain")
        multiplied = sem("multiplied")
        summed = sem("summed")
        gen_mm, gen_ev = sem("gen_mm"), sem("gen_ev")
        ident_cast = sem("ident_cast")
        consts = sem("consts")
        shift_of = dict(t4a=-1, t4b=-1, t5=-1, wo=-1, q00=2, q01=2, t1=3, t6=-1, q10=2, q11=2, k01=2, up=-1,
                        t2=3, mt=1, down=-1, router=-1, qkv0=3, qkv1=3)
        FILLS = list(shift_of)
        filled = {k: sem(f"filled_{k}") for k in FILLS}
        taken = {k: sem(f"taken_{k}") for k in FILLS}
        max_mm, max_red = sem("max_mm"), sem("max_red")
        exp_mm, exp_done = sem("exp_mm"), sem("exp_done")
        pv_mm = sem("pv_mm")
        ctx_out = [sem("ctx_out0"), sem("ctx_out1")]
        sliced = [sem("sliced0"), sem("sliced1")]
        copied = [sem("copied0"), sem("copied1")]
        max_row = [sem("max_row0"), sem("max_row1")]
        kept = [sem("kept0"), sem("kept1")]
        stored = [sem("stored0"), sem("stored1")]
        st1, ag1, ve1, rs1, xn_done = (sem(n) for n in ("st1", "ag1", "ve1", "rs1", "xn_done"))
        st2, ag2, ve2, rs2, xn2_done = (sem(n) for n in ("st2", "ag2", "ve2", "rs2", "xn2_done"))
        bias_in = sem("bias_in")
        rope_m = sem("rope_m")
        roped, cast = sem("roped"), sem("cast")
        part_m, parted = sem("part_m"), sem("parted")
        mpart_m, mparted = sem("mpart_m"), sem("mparted")
        sumd, ctx_norm = sem("sumd"), sem("ctx_norm")
        squared = sem("squared")
        gaps, gap_exp, gated = sem("gaps"), sem("gap_exp"), sem("gated")
        count_mm, counted = sem("count_mm"), sem("counted")
        ex_w, ex_x, ex_up, ex_relu, ex_hid, ex_down, ex_add, ex_out = (
            sem(f"ex_{n}") for n in ("w", "x", "up", "relu", "hid", "down", "add", "out"))

        block = ctx.enter_context(nc.Block())

        def settle(eng):
            eng.wait_ge(ld_id, 16)

        def stacks(t):
            def heads(lo, n):
                return rope_sum[:, t, HD * lo:HD * (lo + n)].rearrange("p (n o d) -> p n o d", n=n, o=1)
            return (q_parts[:, t].rearrange("p n (k d) -> p n k d", k=6),
                    k_parts[:, t, :, 0:STACK].rearrange("p n (k d) -> p n k d", k=6),
                    heads(0, NH), heads(NH, NKV))

        def if_routed(eng):
            eng.wait_ge(counted, 1)
            rows = eng.value_load(routed_n[0:1, 0:1], min_val=0, max_val=P)
            return eng.If(rows > 0)

        def before(name, s):
            at = FILLS.index(name)
            for k in range(2, 2 * len(FILLS) + 1, 2):
                i = at - k
                other = FILLS[i % len(FILLS)]
                b = s.back(-(i // len(FILLS)) - shift_of[other])
                if b.real:
                    return other, b
            return None, None

        @block.sync
        def _(sp):
            sp.dma_start(par_sb[:, 0, :], log_dt.to_broadcast([P, SEQ])).then_inc(ld_dt, 16)
            for half in range(2):
                rows = slice(64 * half, 64 * half + 64)
                sp.dma_start(par_sb[rows, 1, :], inv_a).then_inc(ld_par, 16)
                sp.dma_start(par_sb[rows, 2, :], a_imag).then_inc(ld_par, 16)
                sp.dma_start(par_sb[rows, 3:5, :], b_ri.rearrange("r n h -> n r h")).then_inc(ld_par, 16)
            sp.dma_start(ca, xh.rearrange("r n c h -> (r n) c h")).then_inc(ld_c, 16)
            for half in range(2):
                sp.dma_start(cb[64 * half:64 * half + 64], xh[1 - half]).then_inc(ld_c, 16)
            sp.dma_start(ident[:], ident_d).then_inc(ld_id, 16)
            sp.dma_start(wqkv_sb[:], wqkv.rearrange("(k p) n -> p k n", p=P)).then_inc(ld_w, 16)
            sp.dma_start(wo_sb[:], wo.rearrange("(k p) n -> p k n", p=P)).then_inc(ld_w, 16)
            sp.dma_start(ws1_sb[:], ws1.rearrange("(k p) n -> p k n", p=P)).then_inc(ld_w, 16)
            sp.dma_start(ws2_sb[:], ws2).then_inc(ld_w, 16)
            sp.dma_start(wr_sb[:], wr.rearrange("(k p) n -> p k n", p=P)).then_inc(ld_w, 16)
            sp.dma_start(bqkv_sb[:], bqkv.to_broadcast([P, QKV])).then_inc(ld_w, 16)
            sp.dma_start(bo_sb[:], bo.to_broadcast([P, D])).then_inc(ld_w, 16)
            sp.dma_start(cos_sb[:], cos_t.rearrange("(t p) d -> p t d", p=P)).then_inc(ld_w, 16)
            sp.dma_start(sin_sb[:], sin_t.rearrange("(t p) d -> p t d", p=P)).then_inc(ld_w, 16)

            def load_slice(b):
                if b.static and b.n < 2:
                    sp.wait_ge(gen_ev, GROUPS)
                else:
                    sp.wait_ge(filled["t1"], b.n - 1)
                sp.dma_start(h_slice[b.parity][:], h_feat[:, b.index()].rearrange("p c a t -> p (c a) t")) \
                    .then_inc(sliced[b.parity], 16)

            def step(s):
                c1, b = s.back(-1), s.back(1)
                if s.static and s.n == -3:
                    load_slice(s.back(-3))
                if s.back(-4).real:
                    load_slice(s.back(-4))
                if b.real:
                    sp.wait_ge(taken["t6"], b.n + 1)
                    sp.dma_start(x2_keep[b.index()].rearrange("c p f -> p (c f)"),
                                 x2_t[b.parity][:].rearrange("p k t -> p (k t)")).then_inc(kept[b.parity], 16)
                    sp.wait_ge(taken["down"], b.n + 1)
                    sp.dma_start(out[b.index()].rearrange("c (t p) f -> p (c t) f", p=P),
                                 h_all[:, b.index()].rearrange("p c t f -> p (c t) f")) \
                        .then_inc(stored[b.parity], 16)
                if c1.real:
                    sp.wait_ge(mparted, c1.n + 1)
                    sp.wait_ge(copied[c1.parity], 48 * (c1.half + 1))
                    for k in range(3):
                        sp.dma_start(q_exp[c1.parity][STACK + k:STACK + k + 1], max_parts[c1.parity][:, k, :]) \
                            .then_inc(max_row[c1.parity], 16)

            steps(sp, step)
            sp.wait_ge(stored[0], 16 * CH // 2)
            sp.wait_ge(stored[1], 16 * CH // 2)
            sp.wait_ge(kept[0], 16 * CH // 2)
            sp.wait_ge(kept[1], 16 * CH // 2)

            with if_routed(sp):
                with sp.Fori(0, NE) as e:
                    sp.wait_ge(ex_add, e * CH + 1)
                    sp.dma_start(w1_e, w1[bass.ds(e, 1)].rearrange("e (k p) f -> p (e k) f", p=P)).then_inc(ex_w, 16)
                    sp.dma_start(w2_e, w2[bass.ds(e, 1)].rearrange("e f d -> f (e d)")).then_inc(ex_w, 16)
                    with sp.Fori(0, CH) as c:
                        sp.wait_ge(ex_add, e * CH + c + 1)
                        sp.dma_start(x2_e.rearrange("p k t -> p (k t)"),
                                     x2_keep[bass.ds(c, 1)].rearrange("c p f -> p (c f)")).then_inc(ex_x, 16)
                sp.wait_ge(ex_add, NE * CH + 1)
                sp.dma_start(out.rearrange("c (t p) f -> p (c t) f", p=P),
                             h_all[:].rearrange("p c t f -> p (c t) f")).then_inc(ex_out, 16)
                sp.wait_ge(ex_out, 16)

        @block.tensor
        def _(pe):
            def generate(half):
                r, l1, l2 = (prod[half][k].rearrange("p (h t m) -> p h t m", h=GH, t=2) for k in (0, 2, 3))
                for h in range(GH):
                    for n, l in enumerate((l1, l2)):
                        for t in range(2):
                            last = pe.matmul(misc[half][64 * t:64 * t + 64, 64 * h:64 * h + 64],
                                             r[:, h, t, :], l[:, h, t, :], start=(n == 0), stop=(n == 1))
                last.then_inc(gen_mm, 1)

            def group(g, half):
                pe.wait_ge(multiplied, 4 * g + 4)
                pe.wait_ge(summed, g + 1)
                if not (isinstance(g, int) and g < 2):
                    pe.wait_ge(gen_ev, g - 1)
                generate(half)

            for g in range(2):
                group(g, g)
            with pe.Fori(1, GROUPS // 2) as i:
                for half in range(2):
                    group(2 * i + half, half)
            pe.wait_ge(ld_id, 16)
            pe.wait_ge(ident_cast, 1)
            pe.wait_ge(ld_w, 16 * 9)
            pe.wait_ge(gen_ev, GROUPS)

            def bank(name, s):
                other, b = before(name, s)
                if other:
                    pe.wait_ge(taken[other], b.n + 1)
                return misc[FILLS.index(name) % 2]

            def transpose_tiles(dst, src):
                for t in range(TT):
                    for k in range(2):
                        last = pe.transpose(dst[:, 256 * k + P * t:256 * k + P * (t + 1)],
                                            src[:, t, P * k:P * (k + 1)], ident[:])
                return last

            def heads_of(u):
                return [(j * GQ + u // 2, j, i) for i, j in enumerate((2 * (u % 2), 2 * (u % 2) + 1))]

            def max_scores(b, u):
                if not b.real:
                    return
                if u == 0:
                    for name in ("q00", "q01", "q10", "q11", "k01"):
                        pe.wait_ge(taken[name], b.n + 1)
                if not (b.static and b.n == 0 and u == 0):
                    pe.wait_ge(max_red, UNITS * b.n + u)
                for n, j, i in heads_of(u):
                    for t in range(TT):
                        last = pe.matmul(max_ps[:, i, SEQ * t:SEQ * (t + 1)],
                                         q_max[b.parity][0:STACK, n, P * t:P * (t + 1)],
                                         k_max[b.parity][0:STACK, j, :], start=True, stop=True)
                last.then_inc(max_mm, 1)

            def exp_scores(s, u):
                if not s.real:
                    return
                if u == 0:
                    pe.wait_ge(copied[s.parity], 48 * (s.half + 1))
                    pe.wait_ge(max_row[s.parity], 48 * (s.half + 1))
                if not (s.static and s.n == 0 and u == 0):
                    pe.wait_ge(exp_done, UNITS * s.n + u)
                for n, j, i in heads_of(u):
                    for t in range(TT):
                        last = pe.matmul(exp_ps[:, i, SEQ * t:SEQ * (t + 1)],
                                         k_exp[s.parity][0:KROWS, j, P * t:P * (t + 1)],
                                         q_exp[s.parity][0:KROWS, n, :], start=True, stop=True)
                last.then_inc(exp_mm, 1)

            def values(b, g):
                if not b.real:
                    return
                pe.wait_ge(exp_done, UNITS * b.n + 2 * g + 2)
                if g % 2 == 0 and not (b.static and b.n == 0):
                    pe.wait_ge(ctx_out[g // 2], b.n)
                for t in range(TT):
                    for j in range(NKV):
                        last = pe.matmul(ctx_ps[g // 2][COL * j:COL * (j + 1), SEQ * (g % 2):SEQ * (g % 2 + 1)],
                                         v_exp[b.parity][:, t, j, :], probs[g % 2][:, j, SEQ * t:SEQ * (t + 1)],
                                         start=(t == 0), stop=(t == TT - 1))
                last.then_inc(pv_mm, 1)

            def fill(name, s):
                b = s.back(-shift_of[name])
                if not b.real:
                    return
                dst = bank(name, s)
                if name == "t1":
                    pe.wait_ge(sliced[b.parity], 16 * (b.half + 1))
                    for a in range(A_N):
                        last = pe.transpose(dst[:].rearrange("p (t f) -> p t f", t=2)[:, :, B_N * a:B_N * (a + 1)],
                                            h_slice[b.parity][:, a, :], ident[:])
                elif name == "t2":
                    pe.wait_ge(xn_done, b.n + 1)
                    last = transpose_tiles(dst, xn)
                elif name in ("qkv0", "qkv1"):
                    t = int(name[-1])
                    pe.wait_ge(taken["t2"], b.n + 1)
                    for k in range(2):
                        last = pe.matmul(dst[:, 0:QKV], x_t[:, k, P * t:P * (t + 1)], wqkv_sb[:, k, :],
                                         start=(k == 0), stop=(k == 1))
                elif name in ("q00", "q01", "q10", "q11"):
                    t, half = int(name[1]), int(name[2])
                    pe.wait_ge(parted, 4 * b.n + 2 * t + 2)
                    dst = dst[:].bitcast(BF16)
                    for i in range(NH // 2):
                        last = pe.transpose(dst[0:STACK, P * i:P * (i + 1)], q_parts[:, t, NH // 2 * half + i, :],
                                            ident_b[:])
                elif name == "k01":
                    pe.wait_ge(parted, 4 * b.n + 4)
                    dst = dst[:].bitcast(BF16)
                    for t in range(TT):
                        for j in range(NKV):
                            last = pe.transpose(dst[0:KROWS, SEQ * j + P * t:SEQ * j + P * (t + 1)],
                                                k_parts[:, t, j, :], ident_b[:])
                elif name == "mt":
                    pe.wait_ge(max_red, UNITS * (b.n + 1))
                    for t in range(TT):
                        last = pe.transpose(dst[0:NH, P * t:P * (t + 1)],
                                            neg_max[:, t].rearrange("p j g -> p (j g)"), ident[:])
                elif name in ("t4a", "t4b"):
                    t = int(name == "t4b")
                    pe.wait_ge(ctx_out[0], b.n + 1)
                    pe.wait_ge(ctx_out[1], b.n + 1)
                    for g in range(GQ):
                        last = pe.transpose(dst[:, P * g:P * (g + 1)], ctx_raw[:, g, P * t:P * (t + 1)], ident[:])
                elif name == "t5":
                    pe.wait_ge(taken["t4b"], b.n + 1)
                    last = transpose_tiles(dst, ctx_n[:].rearrange("p t j g d -> p t (j g d)"))
                elif name == "wo":
                    pe.wait_ge(taken["t5"], b.n + 1)
                    for t in range(TT):
                        for k in range(2):
                            last = pe.matmul(dst[:, D * t:D * (t + 1)], ctx_t[:, k, P * t:P * (t + 1)],
                                             wo_sb[:, k, :], start=(k == 0), stop=(k == 1))
                elif name == "t6":
                    pe.wait_ge(xn2_done, b.n + 1)
                    last = transpose_tiles(dst, xn2)
                elif name == "up":
                    pe.wait_ge(taken["t6"], b.n + 1)
                    for k in range(2):
                        last = pe.matmul(dst[:, 0:SEQ], ws1_sb[:, k, :], x2_t[b.parity][:, k, :],
                                         start=(k == 0), stop=(k == 1))
                elif name == "down":
                    pe.wait_ge(squared, b.n + 1)
                    for t in range(TT):
                        last = pe.matmul(dst[:, D * t:D * (t + 1)], hid[:, P * t:P * (t + 1)], ws2_sb[:],
                                         start=True, stop=True)
                elif name == "router":
                    for t in range(TT):
                        for k in range(2):
                            last = pe.matmul(dst[:, NE * t:NE * (t + 1)], x2_t[b.parity][:, k, P * t:P * (t + 1)],
                                             wr_sb[:, k, :], start=(k == 0), stop=(k == 1))
                last.then_inc(filled[name], 1)

            def step(s):
                near, far = s.back(-1), s.back(-2)
                values(s.back(1), 3)
                max_scores(near, 2)
                exp_scores(s, 0)
                fill("t4a", s)
                fill("t4b", s)
                max_scores(near, 3)
                exp_scores(s, 1)
                fill("t5", s)
                max_scores(near, 4)
                values(s, 0)
                exp_scores(s, 2)
                fill("wo", s)
                max_scores(near, 5)
                exp_scores(s, 3)
                fill("q00", s)
                fill("q01", s)
                fill("t1", s)
                values(s, 1)
                max_scores(near, 6)
                exp_scores(s, 4)
                fill("t6", s)
                fill("q10", s)
                fill("q11", s)
                fill("k01", s)
                max_scores(near, 7)
                fill("up", s)
                exp_scores(s, 5)
                fill("t2", s)
                fill("mt", s)
                max_scores(far, 0)
                exp_scores(s, 6)
                fill("down", s)
                fill("router", s)
                values(s, 2)
                max_scores(far, 1)
                exp_scores(s, 7)
                fill("qkv0", s)
                fill("qkv1", s)

            steps(pe, step)

            pe.wait_ge(gated, 1)
            pe.wait_ge(taken["down"], CH)
            pe.wait_ge(taken["router"], CH)
            pe.wait_ge(taken["up"], CH)
            pe.wait_ge(taken["mt"], CH)
            pe.matmul(misc[0][0:1, 0:1], any_gate[:, 0:1], any_gate[:, 1:2], start=True, stop=True) \
                .then_inc(count_mm, 1)
            with if_routed(pe):
                with pe.Fori(0, NE) as e:
                    with pe.Fori(0, CH) as c:
                        n = e * CH + c
                        pe.wait_ge(ex_w, e * 32 + 32)
                        pe.wait_ge(ex_x, n * 16 + 16)
                        pe.wait_ge(ex_add, n + 1)
                        for k in range(2):
                            last = pe.matmul(misc[0][:, 0:SEQ], w1_e[:, k, :], x2_e[:, k, :], start=(k == 0),
                                             stop=(k == 1))
                        last.then_inc(ex_up, 1)
                        pe.wait_ge(ex_hid, n + 1)
                        for t in range(TT):
                            last = pe.matmul(misc[1][:, D * t:D * (t + 1)], hid[:, P * t:P * (t + 1)], w2_e,
                                             start=True, stop=True)
                        last.then_inc(ex_down, 1)

        @block.scalar
        def _(act):
            act.wait_ge(ld_par, 16 * 6)
            act.activation(par_sb[:, 1, :], par_sb[:, 1, :], ACT.Exp).then_inc(exp_par, 1)

            def group(g, half):
                act.wait_ge(gen_mm, g + 1)
                dst = h_feat[:, :, :, g * GH:(g + 1) * GH] if isinstance(g, int) else \
                    h_feat[:, :, :, bass.ds(g * GH, GH)]
                act.copy(dst.rearrange("p c a h -> p h (c a)"),
                         misc[half][:].rearrange("p (h m) -> p h m", h=GH)).then_inc(gen_ev, 1)

            with act.Fori(0, GROUPS // 2) as i:
                for half in range(2):
                    group(2 * i + half, half)

            def take(name, s):
                b = s.back(-shift_of[name])
                if not b.real:
                    return
                src = misc[FILLS.index(name) % 2]
                act.wait_ge(filled[name], b.n + 1)
                if name == "t1":
                    act.copy(h_all[:, b.index()].rearrange("p c t f -> p (c t f)"), src[:]) \
                        .then_inc(taken[name], 1)
                elif name == "t2":
                    if not (b.static and b.n == 0):
                        act.wait_ge(filled["qkv1"], b.n)
                    act.copy(x_t[:].rearrange("p k t -> p (k t)"), src[:]).then_inc(taken[name], 1)
                elif name in ("q00", "q01", "q10", "q11"):
                    t, half = int(name[1]), int(name[2])
                    if name == "q00" and not (b.static and b.n < 2):
                        act.wait_ge(copied[b.parity], 48 * b.half)
                        act.wait_ge(max_mm, UNITS * (b.n - 1))
                    act.copy(q_max[b.parity][0:STACK, NH // 2 * half:NH // 2 * (half + 1), P * t:P * (t + 1)],
                             src[:].bitcast(BF16)[0:STACK].rearrange("p (n t) -> p n t", t=P)) \
                        .then_inc(taken[name], 1)
                elif name == "k01":
                    act.copy(k_max[b.parity][0:KROWS].rearrange("p j t -> p (j t)"),
                             src[:].bitcast(BF16)[0:KROWS]).then_inc(taken[name], 1)
                elif name == "t5":
                    if not (b.static and b.n == 0):
                        act.wait_ge(filled["wo"], b.n)
                    act.copy(ctx_t[:].rearrange("p k t -> p (k t)"), src[:]).then_inc(taken[name], 1)
                elif name == "t6":
                    if not (b.static and b.n < 2):
                        act.wait_ge(filled["router"], b.n - 1)
                        act.wait_ge(kept[b.parity], 16 * b.half)
                    act.copy(x2_t[b.parity][:].rearrange("p k t -> p (k t)"), src[:]).then_inc(taken[name], 1)
                elif name == "up":
                    if not (b.static and b.n == 0):
                        act.wait_ge(squared, b.n)
                    act.activation(hid_relu[:], src[:, 0:SEQ], ACT.Relu).then_inc(taken[name], 1)

            def exponentials(s, u):
                if not s.real:
                    return
                act.wait_ge(exp_mm, UNITS * s.n + u + 1)
                g, half = u // 2, u % 2
                if half == 0 and not (s.static and 4 * s.n + g < 2):
                    act.wait_ge(pv_mm, 4 * s.n + g - 1)
                act.activation(probs[g % 2][:, 2 * half:2 * half + 2, :], exp_ps[:], ACT.Exp, scale=SCALE) \
                    .then_inc(exp_done, 1)

            def move_operands(b):
                if not b.real:
                    return
                for name in ("q00", "q01", "q10", "q11", "k01", "qkv1"):
                    act.wait_ge(taken[name], b.n + 1)
                if not (b.static and b.n < 2):
                    act.wait_ge(pv_mm, 4 * (b.n - 1))
                act.dma_start(q_exp[b.parity][0:STACK], q_max[b.parity][0:STACK]).then_inc(copied[b.parity], 16)
                act.dma_start(k_exp[b.parity][0:KROWS], k_max[b.parity][0:KROWS]).then_inc(copied[b.parity], 16)
                act.dma_start(v_exp[b.parity][:], v_max[b.parity][:]).then_inc(copied[b.parity], 16)

            def cast_first(b, t):
                if not b.real:
                    return
                act.wait_ge(roped, 2 * b.n + t + 1)
                if not (b.static and b.n == 0):
                    act.wait_ge(filled[f"q{t}1"], b.n)
                    act.wait_ge(filled["k01"], b.n)
                qs, ks, q, k = stacks(t)
                wide = lambda m, n: m.to_broadcast([P, m.shape[1], n, HD])
                act.copy(qs[:, :, 0:3], wide(q, 3)).then_inc(cast, 1)
                act.copy(ks[:, :, 0:4:3], wide(k, 2)).then_inc(cast, 1)
                act.copy(ks[:, :, 5:6], k).then_inc(cast, 1)

            def step(s):
                late = s.back(-2)
                move_operands(s.back(-1))
                exponentials(s, 0)
                cast_first(late, 0)
                exponentials(s, 1)
                take("t5", s)
                cast_first(late, 1)
                exponentials(s, 2)
                exponentials(s, 3)
                take("q00", s)
                take("q01", s)
                take("t1", s)
                exponentials(s, 4)
                take("t6", s)
                take("q10", s)
                take("q11", s)
                take("k01", s)
                take("up", s)
                exponentials(s, 5)
                take("t2", s)
                exponentials(s, 6)
                exponentials(s, 7)

            steps(act, step)

            act.wait_ge(gaps, 1)
            act.activation(exp_gap, top2, ACT.Exp).then_inc(gap_exp, 1)
            with if_routed(act):
                with act.Fori(0, NE * CH) as n:
                    act.wait_ge(ex_up, n + 1)
                    act.activation(hid_relu[:], misc[0][:, 0:SEQ], ACT.Relu).then_inc(ex_relu, 1)

        @block.gpsimd
        def _(pool):
            lo, hi = slice(0, P // 2), slice(P // 2, P)
            firsts_of = ((slice(0, P), low, (1.0, 0.0)), (lo, high, (1.0, 0.0)), (hi, high, (0.0, -1.0)))
            for k, (rows, fam, value) in enumerate(firsts_of):
                for r in range(2):
                    pool.memset(fam[rows, 0, r, :], value[r]).then_inc(firsts, 1)
                pool.wait_ge(firsts, 2 * k + 2)
            pool.memset(eps_pow[:], -0.5).then_inc(consts, 1)
            pool.memset(k_parts[:, :, :, STACK:KROWS], 1.0).then_inc(consts, 1)
            for i in range(2):
                pool.memset(v_max[i][:], 0.0).then_inc(consts, 1)
            pool.memset(zeros[:], 0.0).then_inc(consts, 1)
            pool.memset(eps_tile[:], EPS).then_inc(consts, 1)
            pool.wait_ge(consts, 6)
            for i in range(2):
                pool.memset(v_max[i][:, :, :, HD:HD + 1], 1.0).then_inc(consts, 1)
            pool.wait_ge(consts, 8)
            pool.wait_ge(ld_w, 16 * 9)
            pool.wait_ge(ld_id, 16)
            pool.tensor_copy(ident_b[:], ident[:]).then_inc(ident_cast, 1)

            def inverse_std(b, k, ag, ve, rs, used):
                pool.wait_ge(ag, 2 * b.n + 2)
                if not (b.static and b.n == 0):
                    pool.wait_ge(used, b.n)
                pool.tensor_tensor(var_eps[k][:], mean_var[k][:, :, 1], eps_tile[:], ALU.add).then_inc(ve, 1)
                pool.wait_ge(ve, b.n + 1)
                pool.tensor_tensor(rstd[k][:], var_eps[k][:], eps_pow[:], ALU.pow).then_inc(rs, 1)

            def rope(b, t):
                pool.wait_ge(taken[f"qkv{t}"], b.n + 1)
                if not (b.static and b.n == 0):
                    pool.wait_ge(parted, 4 * b.n)
                x = qkv[:, t, 0:QK_COLS]
                heads = x.rearrange("p (h d) -> p h d", d=HD)
                pairs = x.rearrange("p (h d r) -> p h d r", d=HD // 2, r=2)
                rc = rope_c[:, t].rearrange("p (h d) -> p h d", d=HD)
                rs_ = rope_s[:, t].rearrange("p (h d) -> p h d", d=HD)
                n = NH + NKV
                half = HD // 2

                def table(tab, lo, hi):
                    return tab[:, t:t + 1, lo:hi].to_broadcast([P, n, hi - lo])

                pool.tensor_tensor(rc, heads, table(cos_sb, 0, HD), ALU.mult).then_inc(rope_m, 1)
                pool.tensor_tensor(rs_[:, :, 0:half], pairs[:, :, :, 1], table(sin_sb, 0, half), ALU.mult) \
                    .then_inc(rope_m, 1)
                pool.tensor_tensor(rs_[:, :, half:HD], pairs[:, :, :, 0], table(sin_sb, half, HD), ALU.mult) \
                    .then_inc(rope_m, 1)
                pool.wait_ge(rope_m, 3 * (2 * b.n + t) + 3)
                pool.tensor_tensor(rope_sum[:, t], rope_c[:, t], rope_s[:, t], ALU.add).then_inc(roped, 1)

            def split(b, t):
                pool.wait_ge(cast, 3 * (2 * b.n + t) + 3)
                qs, ks, q, k = stacks(t)
                rest_q = rope_c[:, t, 0:NH * HD].rearrange("p (n o d) -> p n o d", n=NH, o=1)
                rest_k = rope_c[:, t, NH * HD:QK_COLS].rearrange("p (n o d) -> p n o d", n=NKV, o=1)
                wide = lambda m: m.to_broadcast([P, m.shape[1], 2, HD])
                pool.tensor_tensor(qs[:, :, 3:5], wide(q), wide(qs[:, :, 0:1]), ALU.subtract).then_inc(part_m, 1)
                pool.tensor_tensor(ks[:, :, 1:5:3], wide(k), wide(ks[:, :, 0:1]), ALU.subtract) \
                    .then_inc(part_m, 1)
                pool.tensor_tensor(rest_q, q, qs[:, :, 0:1], ALU.subtract).then_inc(part_m, 1)
                pool.tensor_tensor(rest_k, k, ks[:, :, 0:1], ALU.subtract).then_inc(part_m, 1)
                pool.wait_ge(part_m, 4 * (2 * b.n + t) + 4)
                pool.tensor_tensor(ks[:, :, 2:3], rest_k, ks[:, :, 1:2], ALU.subtract).then_inc(parted, 1)
                pool.tensor_tensor(qs[:, :, 5:6], rest_q, qs[:, :, 3:4], ALU.subtract).then_inc(parted, 1)

            def split_max(b):
                pool.wait_ge(taken["mt"], b.n + 1)
                if not (b.static and b.n < 2):
                    pool.wait_ge(max_row[b.parity], 48 * b.half)
                m = max_parts[b.parity]
                pool.tensor_tensor(m[:, 0, :], neg_max_t[:], zeros[:], ALU.add).then_inc(mpart_m, 1)
                pool.wait_ge(mpart_m, 3 * b.n + 1)
                pool.tensor_tensor(max_rest[:], neg_max_t[:], m[:, 0, :], ALU.subtract).then_inc(mpart_m, 1)
                pool.wait_ge(mpart_m, 3 * b.n + 2)
                pool.tensor_tensor(m[:, 1, :], max_rest[:], zeros[:], ALU.add).then_inc(mpart_m, 1)
                pool.wait_ge(mpart_m, 3 * b.n + 3)
                pool.tensor_tensor(m[:, 2, :], max_rest[:], m[:, 1, :], ALU.subtract).then_inc(mparted, 1)

            def step(s):
                post, late, pre, scored = s.back(1), s.back(-2), s.back(-3), s.back(-1)
                if late.real:
                    rope(late, 0)
                    rope(late, 1)
                    split(late, 0)
                if post.real:
                    inverse_std(post, 1, ag2, ve2, rs2, xn2_done)
                if late.real:
                    split(late, 1)
                if pre.real:
                    inverse_std(pre, 0, ag1, ve1, rs1, xn_done)
                if scored.real:
                    split_max(scored)
                if pre.real:
                    pool.wait_ge(xn_done, pre.n + 1)
                    h = h_all[:, pre.index()].rearrange("p c t f -> p (c t) f")
                    pool.tensor_tensor(h, h, bo_sb[:].rearrange("p (o f) -> p o f", o=1).to_broadcast([P, TT, D]),
                                       ALU.add).then_inc(bias_in, 1)

            steps(pool, step)

        @block.vector
        def _(dve):
            links = [0]

            def put(ins):
                links[0] += 1
                ins.then_inc(chain, 1)
                return links[0]

            def link(ins):
                dve.wait_ge(chain, put(ins))

            lo, hi = slice(0, P // 2), slice(P // 2, P)
            log_p, a_p, im_p, br_p, bi_p = (par_sb[:, k, :] for k in range(5))
            half_dt, na, b_, one_a, den, s_, s2, whole, rest = (small[:, k, :] for k in range(9))
            power_bits = den.bitcast(I32)

            magic, ln2_hi = 12582912.0, 0.693359375
            ln2_lo = float(np.log(2.0)) - ln2_hi
            dve.wait_ge(ld_dt, 16)
            link(dve.tensor_scalar(log_p, log_p, -87.0, 88.0, ALU.max, ALU.min))
            link(dve.tensor_scalar(whole, log_p, float(1 / np.log(2.0)), magic, ALU.mult, ALU.add))
            link(dve.tensor_scalar(whole, whole, magic, None, ALU.subtract))
            link(dve.scalar_tensor_tensor(out=rest, in0=whole, scalar=-ln2_hi, in1=log_p, op0=ALU.mult, op1=ALU.add))
            link(dve.scalar_tensor_tensor(out=rest, in0=whole, scalar=-ln2_lo, in1=rest, op0=ALU.mult, op1=ALU.add))
            put(dve.tensor_scalar(power_bits, whole, 127.0, float(2 ** 23), ALU.add, ALU.mult))
            factorial = [1.0, 1.0, 2.0, 6.0, 24.0, 120.0, 720.0, 5040.0]
            link(dve.tensor_scalar(half_dt, rest, 1 / factorial[7], None, ALU.mult))
            for k in range(6, 0, -1):
                link(dve.scalar_tensor_tensor(out=half_dt, in0=half_dt, scalar=1 / factorial[k], in1=rest,
                                              op0=ALU.add, op1=ALU.mult))
            link(dve.scalar_tensor_tensor(out=half_dt, in0=half_dt, scalar=1.0, in1=den, op0=ALU.add, op1=ALU.mult))
            link(dve.tensor_scalar(half_dt, half_dt, 0.5, None, ALU.mult))

            dve.wait_ge(ld_par, 16 * 6)
            put(dve.tensor_tensor(b_, im_p, half_dt, ALU.mult))
            dve.wait_ge(exp_par, 1)
            link(dve.tensor_tensor(na, a_p, half_dt, ALU.mult))
            put(dve.tensor_tensor(s2, b_, b_, ALU.mult))
            link(dve.tensor_scalar(one_a, na, 1.0, None, ALU.add))
            put(dve.tensor_tensor(s_, na, na, ALU.mult))
            link(dve.tensor_tensor(den, one_a, one_a, ALU.mult))
            put(dve.tensor_tensor(s_, s_, s2, ALU.add))
            link(dve.tensor_tensor(den, den, s2, ALU.add))
            put(dve.tensor_scalar(s_, s_, -1.0, 1.0, ALU.mult, ALU.add))
            link(dve.reciprocal(one_a, den))
            put(dve.tensor_tensor(low[:, 1, 0, :], s_, one_a, ALU.mult))
            link(dve.scalar_tensor_tensor(out=low[:, 1, 1, :], in0=b_, scalar=2.0, in1=one_a,
                                          op0=ALU.mult, op1=ALU.mult))

            def square(dst, z):
                put(dve.tensor_tensor(tmp_sq[:, 0], z, z, ALU.mult))
                done = put(dve.scalar_tensor_tensor(out=dst[:, 1, :], in0=z[:, 0, :], scalar=2.0, in1=z[:, 1, :],
                                                    op0=ALU.mult, op1=ALU.mult))
                dve.wait_ge(chain, done - 1)
                return put(dve.tensor_tensor(dst[:, 0, :], tmp_sq[:, 0, 0, :], tmp_sq[:, 0, 1, :], ALU.subtract))

            def product(dst, many, one):
                m = many.shape[1]
                shape = [P, m, 2, SEQ]
                re = one[:, 0:1, :].rearrange("p (m r) h -> p m r h", m=1).to_broadcast(shape)
                im = one[:, 1:2, :].rearrange("p (m r) h -> p m r h", m=1).to_broadcast(shape)
                put(dve.tensor_tensor(tmp_re[:, 0:m], many, re, ALU.mult))
                link(dve.tensor_tensor(tmp_im[:, 0:m], many, im, ALU.mult))
                put(dve.tensor_tensor(dst[:, :, 0, :], tmp_re[:, 0:m, 0, :], tmp_im[:, 0:m, 1, :], ALU.subtract))
                return put(dve.tensor_tensor(dst[:, :, 1, :], tmp_re[:, 0:m, 1, :], tmp_im[:, 0:m, 0, :], ALU.add))

            there = lambda count: dve.wait_ge(chain, count)
            w8, w16, w32, w64, w128 = (squares[:, k] for k in range(5))
            dve.wait_ge(firsts, 6)
            there(square(low[:, 2], low[:, 1]))
            w4_at = square(low[:, 4], low[:, 2])
            w3_at = product(low[:, 3:4], low[:, 1:2], low[:, 2])
            there(w4_at)
            w8_at = square(w8, low[:, 4])
            there(w3_at)
            product(low[:, 5:8], low[:, 1:4], low[:, 4])
            there(w8_at)
            w16_at = square(w16, w8)
            put(dve.tensor_copy(high[lo, 1], w8[lo]))
            put(dve.tensor_copy(high[hi, 1, 0, :], w8[hi, 1, :]))
            put(dve.tensor_scalar(high[hi, 1, 1, :], w8[hi, 0, :], -1.0, None, ALU.mult))
            put(dve.tensor_scalar(gain[lo, 0, 0, :], br_p[lo], 2.0, None, ALU.mult))
            put(dve.tensor_scalar(gain[hi, 0, 0, :], br_p[hi], -2.0, None, ALU.mult))
            high1_at = put(dve.tensor_scalar(gain[:, 0, 1, :], bi_p, -2.0, None, ALU.mult))
            there(w16_at)
            w32_at = square(w32, w16)
            there(high1_at)
            high3_at = product(high[:, 2:4], high[:, 0:2], w16)
            there(w32_at)
            w64_at = square(w64, w32)
            there(high3_at)
            product(high[:, 4:8], high[:, 0:4], w32)
            there(w64_at)
            link(dve.tensor_scalar(w64[lo, 1, :], w64[lo, 1, :], -1.0, None, ALU.mult))
            w128_at = square(w128, w64)
            gain1_at = product(gain[:, 1:2], gain[:, 0:1], w64)
            there(w128_at)
            there(gain1_at)
            there(product(gain[:, 2:4], gain[:, 0:2], w128))
            dve.wait_ge(ld_c, 16 * 3)

            def group(g, half):
                if not (isinstance(g, int) and g < 2):
                    dve.wait_ge(gen_mm, g - 1)
                hs = slice(g * 2 * GH, (g + 1) * 2 * GH) if isinstance(g, int) else bass.ds(g * 2 * GH, 2 * GH)
                n = 2 * GH
                for r in range(2):
                    xs = high[:, :, r, hs].rearrange("p (m o) h -> p h m o", o=1).to_broadcast([P, n, 8, 8])
                    ys = low[:, :, r, hs].rearrange("p (o m) h -> p h o m", o=1).to_broadcast([P, n, 8, 8])
                    dve.tensor_tensor(prod[half][r].rearrange("p (h i j) -> p h i j", h=n, i=8), xs, ys,
                                      ALU.mult).then_inc(multiplied, 1)
                for r, c in enumerate((ca, cb)):
                    xs = c[:, :, hs].rearrange("p (c o) h -> p h c o", o=1).to_broadcast([P, n, CH, A_N])
                    ys = gain[:, :, r, hs].rearrange("p (o m) h -> p h o m", o=1).to_broadcast([P, n, CH, A_N])
                    dve.tensor_tensor(prod[half][2 + r].rearrange("p (h c a) -> p h c a", h=n, c=CH), xs, ys,
                                      ALU.mult).then_inc(multiplied, 1)
                dve.wait_ge(multiplied, 4 * g + 2)
                dve.tensor_tensor(prod[half][0], prod[half][0], prod[half][1], ALU.subtract).then_inc(summed, 1)

            for g in range(2):
                group(g, g)
            with dve.Fori(1, GROUPS // 2) as i:
                for half in range(2):
                    group(2 * i + half, half)
            dve.wait_ge(ld_w, 16 * 9)
            dve.wait_ge(consts, 8)

            def statistics(b, k, src, st, ag):
                for t in range(TT):
                    dve.bn_stats(stats[k][:, t, :], src[:, t, :]).then_inc(st, 1)
                dve.wait_ge(st, 2 * b.n + 2)
                if not (b.static and b.n == 0):
                    dve.wait_ge([xn_done, xn2_done][k], b.n)
                dve.memset(carrier[:], 0.0)
                for t in range(TT):
                    dve.bn_aggr(mean_var[k][:, t, :], stats[k][:, t, :]).then_inc(ag, 1)

            def normalize(b, k, dst, src, rs, done):
                dve.wait_ge(rs, b.n + 1)
                for t in range(TT):
                    last = dve.tensor_scalar(dst[:, t, :], src[:, t, :], mean_var[k][:, t, 0:1],
                                             rstd[k][:, t:t + 1], ALU.subtract, ALU.mult)
                last.then_inc(done, 1)

            def tokens_of(b):
                return h_all[:, b.index()].rearrange("p c t f -> p (c t) f")

            def row_max(b, u):
                if not b.real:
                    return
                g, half = u // 2, u % 2
                dve.wait_ge(max_mm, UNITS * b.n + u + 1)
                if u == 0 and not (b.static and b.n == 0):
                    dve.wait_ge(filled["mt"], b.n)
                dve.tensor_reduce(neg_max[:, :, 2 * half:2 * half + 2, g].rearrange("p t j -> p j t"),
                                  max_ps[:].rearrange("p j (t k) -> p j t k", t=TT), AX.X, ALU.max,
                                  negate=True).then_inc(max_red, 1)

            def take_ctx(b, half):
                if not b.real:
                    return
                dve.wait_ge(pv_mm, 4 * b.n + 2 * half + 2)
                if not (b.static and b.n == 0):
                    dve.wait_ge(filled["t4b"], b.n)
                dve.tensor_copy(ctx_raw[:, 2 * half:2 * half + 2, :].rearrange("p g t -> p (g t)"),
                                ctx_ps[half][:]).then_inc(ctx_out[half], 1)

            def take(name, s):
                b = s.back(-shift_of[name])
                if not b.real:
                    return
                src = misc[FILLS.index(name) % 2]
                dve.wait_ge(filled[name], b.n + 1)
                if name in ("down", "wo"):
                    if name == "wo":
                        dve.wait_ge(bias_in, b.n + 1)
                    h = tokens_of(b)
                    dve.tensor_tensor(h, src[:].rearrange("p (t f) -> p t f", t=TT), h, ALU.add) \
                        .then_inc(taken[name], 1)
                elif name in ("t4a", "t4b"):
                    t = int(name == "t4b")
                    heads = src[:].rearrange("p (g j d) -> p g j d", g=GQ, j=NKV)
                    if not (b.static and b.n == 0):
                        dve.wait_ge(filled["t5"], b.n)
                    dve.reciprocal(ctx_sum[:, t], heads[:, :, :, HD]).then_inc(sumd, 1)
                    dve.wait_ge(sumd, 2 * b.n + t + 1)
                    inv = ctx_sum[:, t].rearrange("p g (j o) -> p g j o", o=1).to_broadcast([P, GQ, NKV, HD])
                    dve.tensor_tensor(ctx_n[:, t].rearrange("p j g d -> p g j d"), heads[:, :, :, 0:HD], inv,
                                      ALU.mult).then_inc(taken[name], 1)
                elif name in ("qkv0", "qkv1"):
                    t = int(name[-1])
                    if not (b.static and b.n == 0):
                        dve.wait_ge(rope_m, 6 * b.n)
                    if not (b.static and b.n < 2):
                        dve.wait_ge(copied[b.parity], 48 * b.half)
                    dve.tensor_tensor(qkv[:, t, 0:QK_COLS], src[:, 0:QK_COLS], bqkv_sb[:, 0:QK_COLS], ALU.add)
                    dve.tensor_tensor(v_max[b.parity][:, t, :, 0:HD],
                                      src[:, QK_COLS:QKV].rearrange("p (j d) -> p j d", j=NKV),
                                      bqkv_sb[:, QK_COLS:QKV].rearrange("p (j d) -> p j d", j=NKV),
                                      ALU.add).then_inc(taken[name], 1)
                elif name == "router":
                    dve.tensor_copy(logits[:, b.index(), :].rearrange("p c e -> p (c e)"), src[:, 0:TT * NE]) \
                        .then_inc(taken[name], 1)
                elif name == "mt":
                    if not (b.static and b.n == 0):
                        dve.wait_ge(mparted, b.n)
                    dve.tensor_copy(neg_max_t[:], src[0:NH, 0:SEQ]).then_inc(taken[name], 1)

            def square(b):
                if not b.real:
                    return
                dve.wait_ge(taken["up"], b.n + 1)
                if not (b.static and b.n == 0):
                    dve.wait_ge(filled["down"], b.n)
                dve.tensor_tensor(hid[:], hid_relu[:], hid_relu[:], ALU.mult).then_inc(squared, 1)

            def step(s):
                near, far, pre, post = s.back(-1), s.back(-2), s.back(-3), s.back(1)
                take_ctx(post, 1)
                row_max(near, 2)
                take("t4a", s)
                take("t4b", s)
                row_max(near, 3)
                row_max(near, 4)
                take("wo", s)
                if post.real:
                    settle(dve)
                    dve.wait_ge(taken["wo"], post.n + 1)
                    statistics(post, 1, tokens_of(post), st2, ag2)
                row_max(near, 5)
                if pre.real:
                    settle(dve)
                    dve.wait_ge(taken["t1"], pre.n + 1)
                    statistics(pre, 0, tokens_of(pre), st1, ag1)
                if post.real:
                    if not (post.static and post.n == 0):
                        dve.wait_ge(filled["t6"], post.n)
                    normalize(post, 1, xn2, tokens_of(post), rs2, xn2_done)
                take_ctx(s, 0)
                row_max(near, 6)
                if pre.real:
                    if not (pre.static and pre.n == 0):
                        dve.wait_ge(filled["t2"], pre.n)
                    normalize(pre, 0, xn, tokens_of(pre), rs1, xn_done)
                row_max(near, 7)
                square(post)
                take("mt", s)
                row_max(far, 0)
                take("down", s)
                take("router", s)
                row_max(far, 1)
                take("qkv0", s)
                take("qkv1", s)

            steps(dve, step)

            lg = logits[:].rearrange("p c (t e) -> p (c t) e", e=NE)
            per_tile = lambda m: m.rearrange("p (t o) -> p t o", o=1).to_broadcast([P, tiles, NE])
            dve.wait_ge(taken["router"], CH)
            dve.wait_ge(filled["mt"], CH)
            dve.wait_ge(filled["down"], CH)
            link(dve.tensor_reduce(top1, lg, AX.X, ALU.max))
            link(dve.tensor_tensor(is_top, lg, per_tile(top1), ALU.is_equal))
            link(dve.scalar_tensor_tensor(out=others, in0=is_top, scalar=-3.0e38, in1=lg, op0=ALU.mult,
                                          op1=ALU.add))
            link(dve.tensor_reduce(top2, others, AX.X, ALU.max))
            link(dve.tensor_reduce(n_top, is_top, AX.X, ALU.add))
            link(dve.tensor_scalar(n_top, n_top, 1.0, None, ALU.is_equal))
            dve.tensor_tensor(top2, top2, top1, ALU.subtract).then_inc(gaps, 1)
            dve.wait_ge(gap_exp, 1)
            link(dve.tensor_scalar(exp_gap, exp_gap, 1.0, None, ALU.add))
            link(dve.tensor_scalar(exp_gap, exp_gap, 1.0, None, ALU.is_le))
            link(dve.tensor_tensor(gate, exp_gap, n_top, ALU.mult))
            link(dve.tensor_tensor(weight.rearrange("p (t e) -> p t e", e=NE), is_top, per_tile(gate), ALU.mult))
            link(dve.tensor_reduce(any_gate[:, 0:1], gate, AX.X, ALU.max))
            dve.memset(any_gate[:, 1:2], 1.0).then_inc(gated, 1)
            dve.wait_ge(count_mm, 1)
            dve.tensor_copy(routed_n[:], misc[0][0:1, 0:1]).then_inc(counted, 1)
            with if_routed(dve):
                for i in range(2):
                    dve.wait_ge(stored[i], 16 * CH // 2)
                dve.memset(carrier[:], 0.0).then_inc(ex_add, 1)
                with dve.Fori(0, NE) as e:
                    with dve.Fori(0, CH) as c:
                        n = e * CH + c
                        dve.wait_ge(ex_relu, n + 1)
                        dve.tensor_tensor(hid[:], hid_relu[:], hid_relu[:], ALU.mult).then_inc(ex_hid, 1)
                        dve.wait_ge(ex_down, n + 1)
                        for t in range(TT):
                            h = h_all[:, bass.ds(c, 1), t, :].rearrange("p c f -> p (c f)")
                            ins = dve.scalar_tensor_tensor(
                                out=h, in0=misc[1][:, D * t:D * (t + 1)],
                                scalar=weight[:, bass.ds(c * (TT * NE) + e + t * NE, 1)], in1=h,
                                op0=ALU.mult, op1=ALU.add)
                        ins.then_inc(ex_add, 1)


def kernel(**inputs):
    import numpy as _np
    import concourse.bacc as _bacc
    from concourse import mybir as _mybir
    from concourse.bass_utils import run_bass_kernel_spmd as _run

    def pair_order(a):
        return a.reshape(*a.shape[:-1], 2, 128).swapaxes(-1, -2).reshape(a.shape)

    x = _np.asarray(inputs["x"])
    arrays = {
        "xh": pair_order(x.transpose(3, 2, 0, 1)),
        "log_dt": pair_order(_np.asarray(inputs["L0_tok_log_dt"])[None, :]),
        "inv_a": pair_order(_np.asarray(inputs["L0_tok_inv_A_real"]).T),
        "a_imag": pair_order(_np.asarray(inputs["L0_tok_A_imag"]).T),
        "b_ri": pair_order(_np.asarray(inputs["L0_tok_B_ri"]).transpose(2, 1, 0)),
        "wqkv": _np.concatenate([_np.asarray(inputs[f"L0_attn_W{k}"]) for k in "qkv"]).T,
        "bqkv": _np.concatenate([_np.asarray(inputs[f"L0_attn_b{k}"]) for k in "qkv"])[None, :],
        "wo": _np.asarray(inputs["L0_attn_Wo"]).T,
        "bo": _np.asarray(inputs["L0_attn_bo"])[None, :],
        "ws1": _np.asarray(inputs["L0_ffn_Ws1"]),
        "ws2": _np.asarray(inputs["L0_ffn_Ws2"]),
        "w1": _np.asarray(inputs["L0_ffn_W1"]),
        "w2": _np.asarray(inputs["L0_ffn_W2"]),
        "wr": _np.asarray(inputs["L0_ffn_Wr"]),
    }
    f32 = _np.float32
    inv_freq = (f32(1.0) / f32(10000.0) ** (_np.arange(0, HD, 2, dtype=f32) / f32(HD))).astype(f32)
    angle = _np.arange(SEQ, dtype=f32)[:, None] * inv_freq[None, :]
    arrays["cos_t"] = _np.concatenate([_np.cos(angle)] * 2, -1).astype(f32)
    arrays["sin_t"] = _np.concatenate([-_np.sin(angle), _np.sin(angle)], -1).astype(f32)
    arrays["ident"] = _np.eye(128, dtype=f32)

    nc = _bacc.Bacc("TRN2", target_bir_lowering=False, num_devices=1)
    names, args = {}, []
    for name, a in arrays.items():
        a = _np.ascontiguousarray(a)
        names[f"in_{name}"] = a
        args.append(nc.dram_tensor(f"in_{name}", a.shape, _mybir.dt.from_np(a.dtype), kind="ExternalInput").ap())
    out = nc.dram_tensor("out_0", (CH, SEQ, D), _mybir.dt.float32, kind="ExternalOutput").ap()
    vit_block_kernel(nc, *args, out)
    r = _run(nc, [names], core_ids=[0])
    return r.results[0]["out_0"]
```

```python
from contextlib import ExitStack

import numpy as np

import concourse.bass as bass
from concourse import mybir

F32 = mybir.dt.float32
BF16 = mybir.dt.bfloat16
I32 = mybir.dt.int32
ACT = mybir.ActivationFunctionType
ALU = mybir.AluOpType
AX = mybir.AxisListType

P = 128
CH, SEQ, NS = 16, 256, 64
D = 256
TT = SEQ // P
A_N, B_N = 4, 64
NH, NKV, HD = 16, 4, 16
GQ = NH // NKV
QK_COLS = (NH + NKV) * HD
QKV = QK_COLS + NKV * HD
COL = 32
STACK = 6 * HD
KROWS = STACK + 3
UNITS = NH // 2
SCALE = 1.0 / float(np.sqrt(HD))
EPS = 1e-5
FF = 128
NE = 8
MISC = 3
GH = 8
GROUPS = P // GH
GC = 2 * GH * B_N
SUMMED = 4


class Batch:

    def __init__(self, base, half, shift):
        self.n = base + shift
        self.static = isinstance(base, int)
        self.parity = shift % 2 if not self.static else self.n % 2
        self.half = half + shift // 2 if not self.static else self.n // 2
        self.back = lambda k: Batch(base, half, shift - k)

    @property
    def real(self):
        return not self.static or 0 <= self.n < CH

    def index(self):
        return slice(self.n, self.n + 1) if self.static else bass.ds(self.n, 1)


def steps(eng, step):
    for s in range(-3, 2):
        step(Batch(s, None, 0))
    with eng.Fori(1, CH // 2 - 2) as i:
        for par in range(2):
            step(Batch(2 * i, i, par))
    for s in range(CH - 4, CH + 1):
        step(Batch(s, None, 0))


def vit_block_kernel(nc, xh, log_dt, pole, wqkv, bqkv, wo, bo, ws1, ws2, w1, w2, wr,
                     cos_t, sin_t, ident_d, out):
    with ExitStack() as ctx:
        def sb(name, shape, dt=F32):
            return ctx.enter_context(nc.sbuf_tensor(name, shape, dt))

        def sem(name):
            return ctx.enter_context(nc.semaphore(name))

        h_feat = sb("h_feat", [P, CH, A_N, P])
        h_all = sb("h_all", [P, CH, TT, D])
        region = sb("region", [P, 8192])
        arena = sb("arena", [P, 12032])
        x2_keep = nc.dram_tensor("x2_keep", [CH, P, 2 * SEQ], F32, kind="Internal").ap()
        ident = sb("ident", [P, P])
        ident_b = sb("ident_b", [P, P], BF16)
        wqkv_sb = sb("wqkv_sb", [P, 2, QKV])
        wo_sb = sb("wo_sb", [P, 2, D])
        ws1_sb = sb("ws1_sb", [P, 2, FF])
        ws2_sb = sb("ws2_sb", [P, D])
        wr_sb = sb("wr_sb", [P, 2, NE])
        bqkv_sb = sb("bqkv_sb", [P, QKV])
        bo_sb = sb("bo_sb", [P, D])
        cos_sb = sb("cos_sb", [P, TT, HD])
        sin_sb = sb("sin_sb", [P, TT, HD])
        eps_pow = sb("eps_pow", [P, TT])
        carrier = sb("carrier", [P, 1])
        eps_tile = sb("eps_tile", [P, TT])
        h_slice = [sb(f"h_slice{i}", [P, A_N, P]) for i in range(2)]
        stats = [sb(f"stats{i}", [P, TT, 6]) for i in range(2)]
        mean_var = [sb(f"mean_var{i}", [P, TT, 2]) for i in range(2)]
        var_eps = [sb(f"var_eps{i}", [P, TT]) for i in range(2)]
        rstd = [sb(f"rstd{i}", [P, TT]) for i in range(2)]
        qkv = sb("qkv", [P, TT, QKV])
        rope_sum = sb("rope_sum", [P, TT, QK_COLS])
        zeros = sb("zeros", [NH, SEQ])
        q_parts = sb("q_parts", [P, TT, NH, STACK], BF16)
        k_parts = sb("k_parts", [P, TT, NKV, KROWS], BF16)
        v_max = [sb(f"v_max{i}", [P, TT, NKV, COL]) for i in range(2)]
        v_exp = [sb(f"v_exp{i}", [P, TT, NKV, COL]) for i in range(2)]
        neg_max = sb("neg_max", [P, TT, NKV, GQ])
        neg_max_t = sb("neg_max_t", [NH, SEQ])
        max_rest = sb("max_rest", [NH, SEQ])
        max_parts = [sb(f"max_parts{i}", [NH, 3, SEQ], BF16) for i in range(2)]
        ctx_sum = sb("ctx_sum", [P, TT, GQ, NKV])
        ctx_n = sb("ctx_n", [P, TT, NKV, GQ, HD])
        hid_relu = sb("hid_relu", [FF, SEQ])
        hid = sb("hid", [FF, SEQ])
        logits = sb("logits", [P, CH, TT * NE])

        HH = SEQ // 2

        def family(m, at, src, width=SEQ):
            return src[:, at:at + 2 * width * m].rearrange("p (m r h) -> p m r h", m=m, r=2)

        low = family(8, 0, arena)
        high = family(8, 4096, arena)
        gain = family(A_N, 8192, arena)
        par_sb = arena[:, 10240:10240 + 5 * HH].rearrange("p (k h) -> p k h", k=5)
        hall_flat = h_all[:].rearrange("p c t f -> p (c t f)")
        ca = hall_flat[:, 0:4096].rearrange("p (c h) -> p c h", c=CH)
        cb = hall_flat[:, 4096:8192].rearrange("p (c h) -> p c h", c=CH)
        prod = [[region[:, (4 * i + k) * GC:(4 * i + k + 1) * GC] for k in range(4)] for i in range(2)]
        hf_flat = h_feat[:].rearrange("p c a t -> p (c a t)")
        w64, w128, tmp_sq = (family(1, 2 * HH * k, hf_flat, HH)[:, 0] for k in range(3))
        tmp_re, tmp_im = (family(3, 6 * HH * (1 + k), hf_flat, HH) for k in range(2))
        small = region[:, 0:9 * HH].rearrange("p (k h) -> p k h", k=9)
        q_max, q_exp = ([region[:, 2048 * (2 * k + i):2048 * (2 * k + i + 1)].bitcast(BF16)
                         .rearrange("p (n t) -> p n t", n=NH) for i in range(2)] for k in range(2))
        k_max, k_exp = ([arena[:, 512 * (2 * k + i):512 * (2 * k + i + 1)].bitcast(BF16)
                         .rearrange("p (j t) -> p j t", j=NKV) for i in range(2)] for k in range(2))
        probs = [arena[:, 2048 + 2048 * i:2048 + 2048 * (i + 1)].rearrange("p (j f) -> p j f", j=NKV)
                 for i in range(2)]

        xn, x_t, xn2, ctx_t, x2_t0, x2_t1 = (arena[:, o:o + 512].rearrange("p (k t) -> p k t", k=2)
                                             for o in range(6144, 9216, 512))
        x2_t = [x2_t0, x2_t1]
        ctx_raw = arena[:, 9216:10240].rearrange("p (g t) -> p g t", g=GQ)

        rope_c, rope_s = (arena[:, o:o + TT * QK_COLS].rearrange("p (t f) -> p t f", t=TT)
                          for o in (10240, 10240 + TT * QK_COLS))

        w1_e = arena[:, 0:2 * FF].rearrange("p (k f) -> p k f", k=2)
        w2_e = arena[:, 256:256 + D]
        x2_e = arena[:, 512:1024].rearrange("p (k t) -> p k t", k=2)
        tiles = CH * TT
        route = arena[:, 1024:1024 + 12 * tiles]
        top1, top2, n_top, exp_gap, gate = (route[:, tiles * k:tiles * (k + 1)] for k in range(5))
        is_top = arena[:, 2048:2048 + tiles * NE].rearrange("p (t e) -> p t e", e=NE)
        others = arena[:, 2304:2304 + tiles * NE].rearrange("p (t e) -> p t e", e=NE)
        weight = arena[:, 2560:2560 + tiles * NE]
        any_gate = sb("any_gate", [P, 2])
        routed_n = sb("routed_n", [1, 1], I32)

        max_ps = ctx.enter_context(nc.psum_tensor("max_ps", [P, 2, 512], F32))
        exp_ps = ctx.enter_context(nc.psum_tensor("exp_ps", [P, 2, 512], F32))
        ctx_ps = ctx.enter_context(nc.psum_tensor("ctx_ps", [P, 512], F32))
        misc = [ctx.enter_context(nc.psum_tensor(f"misc{i}", [P, 512], F32)) for i in range(MISC)]

        gen_ps = [max_ps, exp_ps]

        ld_dt, ld_par, ld_c, ld_w, ld_id = (sem(f"ld_{n}") for n in ("dt", "par", "c", "w", "id"))
        exp_par = sem("exp_par")
        firsts = sem("firsts")
        chain = sem("chain")
        families = sem("families")
        spread = sem("spread")
        multiplied = sem("multiplied")
        summed = sem("summed")
        gen_mm, gen_ev = sem("gen_mm"), sem("gen_ev")
        ident_cast = sem("ident_cast")
        consts = sem("consts")
        shift_of = dict(t4a=-1, t4b=-1, t5=-1, wo=-1, q00=2, q01=2, t1=3, q10=2, q11=2, k01=2, t6=-1, mt=1,
                        t2=3, up=-1, down=-1, router=-1, qkv0=3, qkv1=3)
        FILLS = list(shift_of)
        filled = {k: sem(f"filled_{k}") for k in FILLS}
        taken = {k: sem(f"taken_{k}") for k in FILLS}
        max_mm, max_red = sem("max_mm"), sem("max_red")
        exp_mm, exp_done = sem("exp_mm"), sem("exp_done")
        pv_mm = sem("pv_mm")
        ctx_out = [sem("ctx_out0"), sem("ctx_out1")]
        sliced = [sem("sliced0"), sem("sliced1")]
        copied = [sem("copied0"), sem("copied1")]
        max_row = [sem("max_row0"), sem("max_row1")]
        kept = [sem("kept0"), sem("kept1")]
        stored = [sem("stored0"), sem("stored1")]
        st1, ag1, ve1, rs1, xn_done = (sem(n) for n in ("st1", "ag1", "ve1", "rs1", "xn_done"))
        st2, ag2, ve2, rs2, xn2_done = (sem(n) for n in ("st2", "ag2", "ve2", "rs2", "xn2_done"))
        bias_in = sem("bias_in")
        rope_m = sem("rope_m")
        roped, cast = sem("roped"), sem("cast")
        part_m, parted = sem("part_m"), sem("parted")
        mpart_m, mparted = sem("mpart_m"), sem("mparted")
        sumd, ctx_norm = sem("sumd"), sem("ctx_norm")
        squared = sem("squared")
        gaps, gap_exp, gated = sem("gaps"), sem("gap_exp"), sem("gated")
        count_mm, counted = sem("count_mm"), sem("counted")
        ex_w, ex_x, ex_up, ex_relu, ex_hid, ex_down, ex_add, ex_out = (
            sem(f"ex_{n}") for n in ("w", "x", "up", "relu", "hid", "down", "add", "out"))

        block = ctx.enter_context(nc.Block())

        def settle(eng):
            eng.wait_ge(ld_id, 16)

        def stacks(t):
            def heads(lo, n):
                return rope_sum[:, t, HD * lo:HD * (lo + n)].rearrange("p (n o d) -> p n o d", n=n, o=1)
            return (q_parts[:, t].rearrange("p n (k d) -> p n k d", k=6),
                    k_parts[:, t, :, 0:STACK].rearrange("p n (k d) -> p n k d", k=6),
                    heads(0, NH), heads(NH, NKV))

        def if_routed(eng):
            eng.wait_ge(counted, 1)
            rows = eng.value_load(routed_n[0:1, 0:1], min_val=0, max_val=P)
            return eng.If(rows > 0)

        def before(name, s):
            at = FILLS.index(name)
            for k in range(MISC, 2 * len(FILLS) + 1, MISC):
                i = at - k
                other = FILLS[i % len(FILLS)]
                b = s.back(-(i // len(FILLS)) - shift_of[other])
                if b.real:
                    return other, b
            return None, None

        @block.sync
        def _(sp):
            for half in range(2):
                sp.dma_start(par_sb[NS * half:NS * (half + 1), 0, :],
                             log_dt[half:half + 1].to_broadcast([NS, HH])).then_inc(ld_dt, 16)
            sp.dma_start(par_sb[:, 1:5, :], pole).then_inc(ld_par, 16)
            sp.dma_start(ca, xh.rearrange("r n c h -> (r n) c h")).then_inc(ld_c, 16)
            for half in range(2):
                sp.dma_start(cb[64 * half:64 * half + 64], xh[1 - half]).then_inc(ld_c, 16)
            sp.dma_start(ident[:], ident_d).then_inc(ld_id, 16)
            sp.dma_start(wqkv_sb[:], wqkv.rearrange("(k p) n -> p k n", p=P)).then_inc(ld_w, 16)
            sp.dma_start(wo_sb[:], wo.rearrange("(k p) n -> p k n", p=P)).then_inc(ld_w, 16)
            sp.dma_start(ws1_sb[:], ws1.rearrange("(k p) n -> p k n", p=P)).then_inc(ld_w, 16)
            sp.dma_start(ws2_sb[:], ws2).then_inc(ld_w, 16)
            sp.dma_start(wr_sb[:], wr.rearrange("(k p) n -> p k n", p=P)).then_inc(ld_w, 16)
            sp.dma_start(bqkv_sb[:], bqkv.to_broadcast([P, QKV])).then_inc(ld_w, 16)
            sp.dma_start(bo_sb[:], bo.to_broadcast([P, D])).then_inc(ld_w, 16)
            sp.dma_start(cos_sb[:], cos_t.rearrange("(t p) d -> p t d", p=P)).then_inc(ld_w, 16)
            sp.dma_start(sin_sb[:], sin_t.rearrange("(t p) d -> p t d", p=P)).then_inc(ld_w, 16)

            def load_slice(b):
                if b.static and b.n <= 2:
                    sp.wait_ge(gen_ev, 2 * GROUPS)
                else:
                    sp.wait_ge(filled["t1"], b.n - 1)
                sp.dma_start(h_slice[b.parity][:], h_feat[:, b.index()].rearrange("p c a t -> p (c a) t")) \
                    .then_inc(sliced[b.parity], 16)

            def step(s):
                c1, b = s.back(-1), s.back(1)
                if s.back(-4).real:
                    load_slice(s.back(-4))
                if b.real:
                    sp.wait_ge(taken["t6"], b.n + 1)
                    sp.dma_start(x2_keep[b.index()].rearrange("c p f -> p (c f)"),
                                 x2_t[b.parity][:].rearrange("p k t -> p (k t)")).then_inc(kept[b.parity], 16)
                if c1.real:
                    sp.wait_ge(mparted, c1.n + 1)
                    sp.wait_ge(copied[c1.parity], 48 * (c1.half + 1))
                    for k in range(3):
                        sp.dma_start(q_exp[c1.parity][STACK + k:STACK + k + 1], max_parts[c1.parity][:, k, :]) \
                            .then_inc(max_row[c1.parity], 16)
                if b.real:
                    sp.wait_ge(taken["down"], b.n + 1)
                    sp.dma_start(out[b.index()].rearrange("c (t p) f -> p (c t) f", p=P),
                                 h_all[:, b.index()].rearrange("p c t f -> p (c t) f")) \
                        .then_inc(stored[b.parity], 16)

            steps(sp, step)
            sp.wait_ge(stored[0], 16 * CH // 2)
            sp.wait_ge(stored[1], 16 * CH // 2)
            sp.wait_ge(kept[0], 16 * CH // 2)
            sp.wait_ge(kept[1], 16 * CH // 2)

            with if_routed(sp):
                with sp.Fori(0, NE) as e:
                    sp.wait_ge(ex_add, e * CH + 1)
                    sp.dma_start(w1_e, w1[bass.ds(e, 1)].rearrange("e (k p) f -> p (e k) f", p=P)).then_inc(ex_w, 16)
                    sp.dma_start(w2_e, w2[bass.ds(e, 1)].rearrange("e f d -> f (e d)")).then_inc(ex_w, 16)
                    with sp.Fori(0, CH) as c:
                        sp.wait_ge(ex_add, e * CH + c + 1)
                        sp.dma_start(x2_e.rearrange("p k t -> p (k t)"),
                                     x2_keep[bass.ds(c, 1)].rearrange("c p f -> p (c f)")).then_inc(ex_x, 16)
                sp.wait_ge(ex_add, NE * CH + 1)
                sp.dma_start(out.rearrange("c (t p) f -> p (c t) f", p=P),
                             h_all[:].rearrange("p c t f -> p (c t) f")).then_inc(ex_out, 16)
                sp.wait_ge(ex_out, 16)

        @block.tensor
        def _(pe):
            def generate(g, half):
                r1, r2, l1, l2 = (prod[half][k].rearrange("p (h m) -> p h m", h=GH) for k in range(4))
                banks = gen_ps[half][:].rearrange("p b (h m) -> p (b h) m", h=GH // 2)
                for h in reversed(range(GH)):
                    if h == SUMMED - 1:
                        pe.wait_ge(summed, g + 1)
                    pairs = [(r1, l1), (r1, l2)] + [(r2, l1), (r2, l2)] * (h >= SUMMED)
                    for n, (r, l) in enumerate(pairs):
                        last = pe.matmul(banks[:, h, :], r[:, h, :], l[:, h, :], start=(n == 0),
                                         stop=(n == len(pairs) - 1))
                last.then_inc(gen_mm, 1)

            def group(g, half):
                pe.wait_ge(multiplied, 4 * g + 4)
                if not (isinstance(g, int) and g < 2):
                    pe.wait_ge(gen_ev, 2 * g - 2)
                generate(g, half)

            for g in range(2):
                group(g, g)
            with pe.Fori(1, GROUPS // 2) as i:
                for half in range(2):
                    group(2 * i + half, half)
            pe.wait_ge(ld_id, 16)
            pe.wait_ge(ident_cast, 1)
            pe.wait_ge(ld_w, 16 * 9)
            pe.wait_ge(gen_ev, 2 * GROUPS)

            def bank(name, s):
                other, b = before(name, s)
                if other:
                    pe.wait_ge(taken[other], b.n + 1)
                return misc[FILLS.index(name) % MISC]

            def transpose_tiles(dst, src):
                for t in range(TT):
                    for k in range(2):
                        last = pe.transpose(dst[:, 256 * k + P * t:256 * k + P * (t + 1)],
                                            src[:, t, P * k:P * (k + 1)], ident[:])
                return last

            def heads_of(u):
                return [(j * GQ + u // 2, j, i) for i, j in enumerate((2 * (u % 2), 2 * (u % 2) + 1))]

            def max_scores(b, u):
                if not b.real:
                    return
                if u == 0:
                    for name in ("q00", "q01", "q10", "q11", "k01"):
                        pe.wait_ge(taken[name], b.n + 1)
                for n, j, i in heads_of(u):
                    if not (b.static and b.n == 0 and u == 0):
                        pe.wait_ge(max_red, NH * b.n + 2 * u + i - 1)
                    for t in range(TT):
                        last = pe.matmul(max_ps[:, i, SEQ * t:SEQ * (t + 1)],
                                         q_max[b.parity][0:STACK, n, P * t:P * (t + 1)],
                                         k_max[b.parity][0:STACK, j, :], start=True, stop=True)
                    last.then_inc(max_mm, 1)

            def exp_scores(s, u):
                if not s.real:
                    return
                if u == 0:
                    pe.wait_ge(copied[s.parity], 48 * (s.half + 1))
                    pe.wait_ge(max_row[s.parity], 48 * (s.half + 1))
                if not (s.static and s.n == 0 and u == 0):
                    pe.wait_ge(exp_done, UNITS * s.n + u)
                for n, j, i in heads_of(u):
                    for t in range(TT):
                        last = pe.matmul(exp_ps[:, i, SEQ * t:SEQ * (t + 1)],
                                         k_exp[s.parity][0:KROWS, j, P * t:P * (t + 1)],
                                         q_exp[s.parity][0:KROWS, n, :], start=True, stop=True)
                last.then_inc(exp_mm, 1)

            def values(b, g):
                if not b.real:
                    return
                pe.wait_ge(exp_done, UNITS * b.n + 2 * g + 2)
                if g == 2:
                    pe.wait_ge(ctx_out[0], b.n + 1)
                elif g == 0 and not (b.static and b.n == 0):
                    pe.wait_ge(ctx_out[1], b.n)
                for t in range(TT):
                    for j in range(NKV):
                        last = pe.matmul(ctx_ps[COL * j:COL * (j + 1), SEQ * (g % 2):SEQ * (g % 2 + 1)],
                                         v_exp[b.parity][:, t, j, :], probs[g % 2][:, j, SEQ * t:SEQ * (t + 1)],
                                         start=(t == 0), stop=(t == TT - 1))
                last.then_inc(pv_mm, 1)

            def fill(name, s):
                b = s.back(-shift_of[name])
                if not b.real:
                    return
                dst = bank(name, s)
                if name == "t1":
                    direct = b.static and b.n == 0
                    if not direct:
                        pe.wait_ge(sliced[b.parity], 16 * (b.half + b.parity))
                    for a in range(A_N):
                        last = pe.transpose(dst[:].rearrange("p (t f) -> p t f", t=2)[:, :, B_N * a:B_N * (a + 1)],
                                            h_feat[:, 0, a, :] if direct else h_slice[b.parity][:, a, :],
                                            ident[:])
                elif name == "t2":
                    pe.wait_ge(xn_done, b.n + 1)
                    last = transpose_tiles(dst, xn)
                elif name in ("qkv0", "qkv1"):
                    t = int(name[-1])
                    pe.wait_ge(taken["t2"], b.n + 1)
                    for k in range(2):
                        last = pe.matmul(dst[:, 0:QKV], x_t[:, k, P * t:P * (t + 1)], wqkv_sb[:, k, :],
                                         start=(k == 0), stop=(k == 1))
                elif name in ("q00", "q01", "q10", "q11"):
                    t, half = int(name[1]), int(name[2])
                    pe.wait_ge(parted, 4 * b.n + 2 * t + 2)
                    dst = dst[:].bitcast(BF16)
                    for i in range(NH // 2):
                        last = pe.transpose(dst[0:STACK, P * i:P * (i + 1)], q_parts[:, t, NH // 2 * half + i, :],
                                            ident_b[:])
                elif name == "k01":
                    pe.wait_ge(parted, 4 * b.n + 4)
                    dst = dst[:].bitcast(BF16)
                    for t in range(TT):
                        for j in range(NKV):
                            last = pe.transpose(dst[0:KROWS, SEQ * j + P * t:SEQ * j + P * (t + 1)],
                                                k_parts[:, t, j, :], ident_b[:])
                elif name == "mt":
                    pe.wait_ge(max_red, NH * (b.n + 1))
                    for t in range(TT):
                        last = pe.transpose(dst[0:NH, P * t:P * (t + 1)],
                                            neg_max[:, t].rearrange("p j g -> p (j g)"), ident[:])
                elif name in ("t4a", "t4b"):
                    t = int(name == "t4b")
                    pe.wait_ge(ctx_out[0], b.n + 1)
                    pe.wait_ge(ctx_out[1], b.n + 1)
                    for g in range(GQ):
                        last = pe.transpose(dst[:, P * g:P * (g + 1)], ctx_raw[:, g, P * t:P * (t + 1)], ident[:])
                elif name == "t5":
                    pe.wait_ge(taken["t4b"], b.n + 1)
                    last = transpose_tiles(dst, ctx_n[:].rearrange("p t j g d -> p t (j g d)"))
                elif name == "wo":
                    pe.wait_ge(taken["t5"], b.n + 1)
                    for t in range(TT):
                        for k in range(2):
                            last = pe.matmul(dst[:, D * t:D * (t + 1)], ctx_t[:, k, P * t:P * (t + 1)],
                                             wo_sb[:, k, :], start=(k == 0), stop=(k == 1))
                elif name == "t6":
                    pe.wait_ge(xn2_done, b.n + 1)
                    last = transpose_tiles(dst, xn2)
                elif name == "up":
                    pe.wait_ge(taken["t6"], b.n + 1)
                    for k in range(2):
                        last = pe.matmul(dst[:, 0:SEQ], ws1_sb[:, k, :], x2_t[b.parity][:, k, :],
                                         start=(k == 0), stop=(k == 1))
                elif name == "down":
                    pe.wait_ge(squared, b.n + 1)
                    for t in range(TT):
                        last = pe.matmul(dst[:, D * t:D * (t + 1)], hid[:, P * t:P * (t + 1)], ws2_sb[:],
                                         start=True, stop=True)
                elif name == "router":
                    for t in range(TT):
                        for k in range(2):
                            last = pe.matmul(dst[:, NE * t:NE * (t + 1)], x2_t[b.parity][:, k, P * t:P * (t + 1)],
                                             wr_sb[:, k, :], start=(k == 0), stop=(k == 1))
                last.then_inc(filled[name], 1)

            def step(s):
                near, far = s.back(-1), s.back(-2)
                max_scores(near, 2)
                values(s.back(1), 3)
                exp_scores(s, 0)
                max_scores(near, 3)
                fill("t4a", s)
                exp_scores(s, 1)
                fill("t4b", s)
                fill("t5", s)
                exp_scores(s, 2)
                max_scores(near, 4)
                fill("wo", s)
                max_scores(near, 5)
                fill("q00", s)
                exp_scores(s, 3)
                values(s, 0)
                fill("q01", s)
                values(s, 1)
                fill("t1", s)
                max_scores(near, 6)
                fill("q10", s)
                exp_scores(s, 4)
                fill("q11", s)
                max_scores(near, 7)
                fill("k01", s)
                fill("t6", s)
                exp_scores(s, 5)
                fill("mt", s)
                max_scores(far, 0)
                fill("t2", s)
                fill("up", s)
                values(s, 2)
                exp_scores(s, 6)
                fill("down", s)
                fill("router", s)
                max_scores(far, 1)
                fill("qkv0", s)
                exp_scores(s, 7)
                fill("qkv1", s)

            steps(pe, step)

            pe.wait_ge(gated, 1)
            pe.wait_ge(taken["down"], CH)
            pe.wait_ge(taken["router"], CH)
            pe.wait_ge(taken["up"], CH)
            pe.wait_ge(taken["mt"], CH)
            pe.matmul(misc[0][0:1, 0:1], any_gate[:, 0:1], any_gate[:, 1:2], start=True, stop=True) \
                .then_inc(count_mm, 1)
            with if_routed(pe):
                with pe.Fori(0, NE) as e:
                    with pe.Fori(0, CH) as c:
                        n = e * CH + c
                        pe.wait_ge(ex_w, e * 32 + 32)
                        pe.wait_ge(ex_x, n * 16 + 16)
                        pe.wait_ge(ex_add, n + 1)
                        for k in range(2):
                            last = pe.matmul(misc[0][:, 0:SEQ], w1_e[:, k, :], x2_e[:, k, :], start=(k == 0),
                                             stop=(k == 1))
                        last.then_inc(ex_up, 1)
                        pe.wait_ge(ex_hid, n + 1)
                        for t in range(TT):
                            last = pe.matmul(misc[1][:, D * t:D * (t + 1)], hid[:, P * t:P * (t + 1)], w2_e,
                                             start=True, stop=True)
                        last.then_inc(ex_down, 1)

        @block.scalar
        def _(act):
            act.wait_ge(ld_par, 16)
            act.activation(par_sb[:, 1, :], par_sb[:, 1, :], ACT.Exp).then_inc(exp_par, 1)

            lo, hi = slice(0, NS), slice(NS, P)
            first, second = slice(0, HH), slice(HH, SEQ)
            act.wait_ge(firsts, 4)
            act.wait_ge(families, 1)
            act.copy(low[hi, 1:8, :, second], low[hi, 1:8, :, first]).then_inc(spread, 1)
            act.wait_ge(spread, 1)
            act.copy(low[hi, 1:8, :, first], low[lo, 1:8, :, first]).then_inc(spread, 1)
            act.wait_ge(families, 2)
            act.mul(high[hi, :, 0, second], high[hi, :, 1, first], -1.0).then_inc(spread, 1)
            act.copy(high[hi, :, 1, second], high[hi, :, 0, first]).then_inc(spread, 1)
            act.wait_ge(spread, 4)
            act.mul(high[hi, :, 0, first], high[lo, :, 1, first], -1.0).then_inc(spread, 1)
            act.copy(high[hi, :, 1, first], high[lo, :, 0, first]).then_inc(spread, 1)
            act.wait_ge(families, 3)
            act.mul(gain[hi, :, 0, second], gain[hi, :, 0, first], -1.0).then_inc(spread, 1)
            act.copy(gain[hi, :, 1, second], gain[hi, :, 1, first]).then_inc(spread, 1)
            act.wait_ge(spread, 8)
            act.mul(gain[hi, :, 0, first], gain[lo, :, 0, first], -1.0).then_inc(spread, 1)
            act.copy(gain[hi, :, 1, first], gain[lo, :, 1, first]).then_inc(spread, 1)
            act.wait_ge(spread, 10)
            act.copy(low[lo, 1:8, :, second], low[hi, 1:8, :, second]).then_inc(spread, 1)
            act.copy(high[lo, :, 0, second], high[hi, :, 1, second]).then_inc(spread, 1)
            act.mul(high[lo, :, 1, second], high[hi, :, 0, second], -1.0).then_inc(spread, 1)
            act.mul(gain[lo, :, 0, second], gain[hi, :, 0, second], -1.0).then_inc(spread, 1)
            act.copy(gain[lo, :, 1, second], gain[hi, :, 1, second]).then_inc(spread, 1)

            def group(g, half):
                act.wait_ge(gen_mm, g + 1)
                banks = gen_ps[half][:].rearrange("p b (h m) -> p (b h) m", h=GH // 2)
                for t in range(TT):
                    rows = slice(B_N * t, B_N * (t + 1))
                    dst = h_feat[rows, :, :, g * GH:(g + 1) * GH] if isinstance(g, int) else \
                        h_feat[rows, :, :, bass.ds(g * GH, GH)]
                    act.copy(dst.rearrange("p c a h -> p h (c a)"), banks[rows, :, 64 * t:64 * t + 64]) \
                        .then_inc(gen_ev, 1)

            with act.Fori(0, GROUPS // 2) as i:
                for half in range(2):
                    group(2 * i + half, half)

            def take(name, s):
                b = s.back(-shift_of[name])
                if not b.real:
                    return
                src = misc[FILLS.index(name) % MISC]
                act.wait_ge(filled[name], b.n + 1)
                if name == "t1":
                    act.copy(h_all[:, b.index()].rearrange("p c t f -> p (c t f)"), src[:]) \
                        .then_inc(taken[name], 1)
                elif name == "t2":
                    if not (b.static and b.n == 0):
                        act.wait_ge(filled["qkv1"], b.n)
                    act.copy(x_t[:].rearrange("p k t -> p (k t)"), src[:]).then_inc(taken[name], 1)
                elif name in ("q00", "q01", "q10", "q11"):
                    t, half = int(name[1]), int(name[2])
                    if name == "q00" and not (b.static and b.n < 2):
                        act.wait_ge(copied[b.parity], 48 * b.half)
                        act.wait_ge(max_mm, NH * (b.n - 1))
                    act.copy(q_max[b.parity][0:STACK, NH // 2 * half:NH // 2 * (half + 1), P * t:P * (t + 1)],
                             src[:].bitcast(BF16)[0:STACK].rearrange("p (n t) -> p n t", t=P)) \
                        .then_inc(taken[name], 1)
                elif name == "k01":
                    act.copy(k_max[b.parity][0:KROWS].rearrange("p j t -> p (j t)"),
                             src[:].bitcast(BF16)[0:KROWS]).then_inc(taken[name], 1)
                elif name == "t5":
                    if not (b.static and b.n == 0):
                        act.wait_ge(filled["wo"], b.n)
                    act.copy(ctx_t[:].rearrange("p k t -> p (k t)"), src[:]).then_inc(taken[name], 1)
                elif name == "t6":
                    if not (b.static and b.n < 2):
                        act.wait_ge(filled["router"], b.n - 1)
                        act.wait_ge(kept[b.parity], 16 * b.half)
                    act.copy(x2_t[b.parity][:].rearrange("p k t -> p (k t)"), src[:]).then_inc(taken[name], 1)
                elif name == "up":
                    if not (b.static and b.n == 0):
                        act.wait_ge(squared, b.n)
                    act.activation(hid_relu[:], src[:, 0:SEQ], ACT.Relu).then_inc(taken[name], 1)

            def exponentials(s, u):
                if not s.real:
                    return
                act.wait_ge(exp_mm, UNITS * s.n + u + 1)
                g, half = u // 2, u % 2
                if half == 0 and not (s.static and 4 * s.n + g < 2):
                    act.wait_ge(pv_mm, 4 * s.n + g - 1)
                act.activation(probs[g % 2][:, 2 * half:2 * half + 2, :], exp_ps[:], ACT.Exp, scale=SCALE) \
                    .then_inc(exp_done, 1)

            def move_operands(b):
                if not b.real:
                    return
                for name in ("q00", "q01", "q10", "q11", "k01", "qkv1"):
                    act.wait_ge(taken[name], b.n + 1)
                if not (b.static and b.n < 2):
                    act.wait_ge(pv_mm, 4 * (b.n - 1))
                act.dma_start(q_exp[b.parity][0:STACK], q_max[b.parity][0:STACK]).then_inc(copied[b.parity], 16)
                act.dma_start(k_exp[b.parity][0:KROWS], k_max[b.parity][0:KROWS]).then_inc(copied[b.parity], 16)
                act.dma_start(v_exp[b.parity][:], v_max[b.parity][:]).then_inc(copied[b.parity], 16)

            def cast_first(b, t):
                if not b.real:
                    return
                act.wait_ge(roped, 2 * b.n + t + 1)
                if not (b.static and b.n == 0):
                    act.wait_ge(filled[f"q{t}1"], b.n)
                    act.wait_ge(filled["k01"], b.n)
                qs, ks, q, k = stacks(t)
                wide = lambda m, n: m.to_broadcast([P, m.shape[1], n, HD])
                act.copy(qs[:, :, 0:3], wide(q, 3)).then_inc(cast, 1)
                act.copy(ks[:, :, 0:4:3], wide(k, 2)).then_inc(cast, 1)
                act.copy(ks[:, :, 5:6], k).then_inc(cast, 1)

            def step(s):
                exponentials(s, 0)
                cast_first(s.back(-2), 0)
                move_operands(s.back(-1))
                exponentials(s, 1)
                take("t5", s)
                cast_first(s.back(-2), 1)
                exponentials(s, 2)
                exponentials(s, 3)
                take("q00", s)
                take("q01", s)
                take("t1", s)
                take("q10", s)
                exponentials(s, 4)
                take("q11", s)
                take("k01", s)
                take("t6", s)
                exponentials(s, 5)
                take("t2", s)
                take("up", s)
                exponentials(s, 6)
                exponentials(s, 7)

            steps(act, step)

            act.wait_ge(gaps, 1)
            act.activation(exp_gap, top2, ACT.Exp).then_inc(gap_exp, 1)
            with if_routed(act):
                with act.Fori(0, NE * CH) as n:
                    act.wait_ge(ex_up, n + 1)
                    act.activation(hid_relu[:], misc[0][:, 0:SEQ], ACT.Relu).then_inc(ex_relu, 1)

        @block.gpsimd
        def _(pool):
            for fam, cols in ((low, slice(0, SEQ)), (high, slice(0, HH))):
                for r, value in enumerate((1.0, 0.0)):
                    pool.memset(fam[:, 0, r, cols], value).then_inc(firsts, 1)
            pool.memset(eps_pow[:], -0.5).then_inc(consts, 1)
            pool.memset(k_parts[:, :, :, STACK:KROWS], 1.0).then_inc(consts, 1)
            for i in range(2):
                pool.memset(v_max[i][:], 0.0).then_inc(consts, 1)
            pool.memset(zeros[:], 0.0).then_inc(consts, 1)
            pool.memset(eps_tile[:], EPS).then_inc(consts, 1)
            pool.wait_ge(consts, 6)
            for i in range(2):
                pool.memset(v_max[i][:, :, :, HD:HD + 1], 1.0).then_inc(consts, 1)
            pool.wait_ge(consts, 8)
            pool.wait_ge(ld_w, 16 * 9)
            pool.wait_ge(ld_id, 16)
            pool.tensor_copy(ident_b[:], ident[:]).then_inc(ident_cast, 1)

            def inverse_std(b, k, ag, ve, rs, used):
                if not b.real:
                    return
                pool.wait_ge(ag, 2 * b.n + 2)
                if not (b.static and b.n == 0):
                    pool.wait_ge(used, b.n)
                pool.tensor_tensor(var_eps[k][:], mean_var[k][:, :, 1], eps_tile[:], ALU.add).then_inc(ve, 1)
                pool.wait_ge(ve, b.n + 1)
                pool.tensor_tensor(rstd[k][:], var_eps[k][:], eps_pow[:], ALU.pow).then_inc(rs, 1)

            def rope(b, t):
                if not b.real:
                    return
                pool.wait_ge(taken[f"qkv{t}"], b.n + 1)
                if not (b.static and b.n == 0):
                    pool.wait_ge(parted, 4 * b.n)
                x = qkv[:, t, 0:QK_COLS]
                heads = x.rearrange("p (h d) -> p h d", d=HD)
                pairs = x.rearrange("p (h d r) -> p h d r", d=HD // 2, r=2)
                rc = rope_c[:, t].rearrange("p (h d) -> p h d", d=HD)
                rs_ = rope_s[:, t].rearrange("p (h d) -> p h d", d=HD)
                n = NH + NKV
                half = HD // 2

                def table(tab, lo, hi):
                    return tab[:, t:t + 1, lo:hi].to_broadcast([P, n, hi - lo])

                pool.tensor_tensor(rc, heads, table(cos_sb, 0, HD), ALU.mult).then_inc(rope_m, 1)
                pool.tensor_tensor(rs_[:, :, 0:half], pairs[:, :, :, 1], table(sin_sb, 0, half), ALU.mult) \
                    .then_inc(rope_m, 1)
                pool.tensor_tensor(rs_[:, :, half:HD], pairs[:, :, :, 0], table(sin_sb, half, HD), ALU.mult) \
                    .then_inc(rope_m, 1)
                pool.wait_ge(rope_m, 3 * (2 * b.n + t) + 3)
                pool.tensor_tensor(rope_sum[:, t], rope_c[:, t], rope_s[:, t], ALU.add).then_inc(roped, 1)

            def split(b, t):
                if not b.real:
                    return
                pool.wait_ge(cast, 3 * (2 * b.n + t) + 3)
                qs, ks, q, k = stacks(t)
                rest_q = rope_c[:, t, 0:NH * HD].rearrange("p (n o d) -> p n o d", n=NH, o=1)
                rest_k = rope_c[:, t, NH * HD:QK_COLS].rearrange("p (n o d) -> p n o d", n=NKV, o=1)
                wide = lambda m: m.to_broadcast([P, m.shape[1], 2, HD])
                pool.tensor_tensor(qs[:, :, 3:5], wide(q), wide(qs[:, :, 0:1]), ALU.subtract).then_inc(part_m, 1)
                pool.tensor_tensor(ks[:, :, 1:5:3], wide(k), wide(ks[:, :, 0:1]), ALU.subtract) \
                    .then_inc(part_m, 1)
                pool.tensor_tensor(rest_q, q, qs[:, :, 0:1], ALU.subtract).then_inc(part_m, 1)
                pool.tensor_tensor(rest_k, k, ks[:, :, 0:1], ALU.subtract).then_inc(part_m, 1)
                pool.wait_ge(part_m, 4 * (2 * b.n + t) + 4)
                pool.tensor_tensor(ks[:, :, 2:3], rest_k, ks[:, :, 1:2], ALU.subtract).then_inc(parted, 1)
                pool.tensor_tensor(qs[:, :, 5:6], rest_q, qs[:, :, 3:4], ALU.subtract).then_inc(parted, 1)

            def add_bias(b):
                if not b.real:
                    return
                pool.wait_ge(xn_done, b.n + 1)
                h = h_all[:, b.index()].rearrange("p c t f -> p (c t) f")
                pool.tensor_tensor(h, h, bo_sb[:].rearrange("p (o f) -> p o f", o=1).to_broadcast([P, TT, D]),
                                   ALU.add).then_inc(bias_in, 1)

            def split_max(b):
                if not b.real:
                    return
                pool.wait_ge(taken["mt"], b.n + 1)
                if not (b.static and b.n < 2):
                    pool.wait_ge(max_row[b.parity], 48 * b.half)
                m = max_parts[b.parity]
                pool.tensor_tensor(m[:, 0, :], neg_max_t[:], zeros[:], ALU.add).then_inc(mpart_m, 1)
                pool.wait_ge(mpart_m, 3 * b.n + 1)
                pool.tensor_tensor(max_rest[:], neg_max_t[:], m[:, 0, :], ALU.subtract).then_inc(mpart_m, 1)
                pool.wait_ge(mpart_m, 3 * b.n + 2)
                pool.tensor_tensor(m[:, 1, :], max_rest[:], zeros[:], ALU.add).then_inc(mpart_m, 1)
                pool.wait_ge(mpart_m, 3 * b.n + 3)
                pool.tensor_tensor(m[:, 2, :], max_rest[:], m[:, 1, :], ALU.subtract).then_inc(mparted, 1)

            def step(s):
                late, pre, post = s.back(-2), s.back(-3), s.back(1)
                rope(late, 0)
                rope(late, 1)
                split(late, 0)
                split(late, 1)
                inverse_std(post, 1, ag2, ve2, rs2, xn2_done)
                inverse_std(pre, 0, ag1, ve1, rs1, xn_done)
                add_bias(pre)
                split_max(s.back(-1))

            steps(pool, step)

        @block.vector
        def _(dve):
            links = [0]

            def put(ins):
                links[0] += 1
                ins.then_inc(chain, 1)
                return links[0]

            def link(ins):
                dve.wait_ge(chain, put(ins))

            first = slice(0, HH)
            log_p, a_p, im_p, br_p, bi_p = (par_sb[:, k, :] for k in range(5))
            half_dt, na, b_, one_a, den, s_, s2, whole, rest = (small[:, k, :] for k in range(9))
            power_bits = den.bitcast(I32)

            magic, ln2_hi = 12582912.0, 0.693359375
            ln2_lo = float(np.log(2.0)) - ln2_hi
            dve.wait_ge(ld_dt, 32)
            link(dve.tensor_scalar(log_p, log_p, -87.0, 88.0, ALU.max, ALU.min))
            link(dve.tensor_scalar(whole, log_p, float(1 / np.log(2.0)), magic, ALU.mult, ALU.add))
            link(dve.tensor_scalar(whole, whole, magic, None, ALU.subtract))
            link(dve.scalar_tensor_tensor(out=rest, in0=whole, scalar=-ln2_hi, in1=log_p, op0=ALU.mult, op1=ALU.add))
            link(dve.scalar_tensor_tensor(out=rest, in0=whole, scalar=-ln2_lo, in1=rest, op0=ALU.mult, op1=ALU.add))
            put(dve.tensor_scalar(power_bits, whole, 127.0, float(2 ** 23), ALU.add, ALU.mult))
            factorial = [1.0, 1.0, 2.0, 6.0, 24.0, 120.0, 720.0, 5040.0]
            link(dve.tensor_scalar(half_dt, rest, 1 / factorial[7], None, ALU.mult))
            for k in range(6, 0, -1):
                link(dve.scalar_tensor_tensor(out=half_dt, in0=half_dt, scalar=1 / factorial[k], in1=rest,
                                              op0=ALU.add, op1=ALU.mult))
            link(dve.scalar_tensor_tensor(out=half_dt, in0=half_dt, scalar=1.0, in1=den, op0=ALU.add, op1=ALU.mult))
            link(dve.tensor_scalar(half_dt, half_dt, 0.5, None, ALU.mult))

            dve.wait_ge(ld_par, 16)
            put(dve.tensor_tensor(b_, im_p, half_dt, ALU.mult))
            dve.wait_ge(exp_par, 1)
            link(dve.tensor_tensor(na, a_p, half_dt, ALU.mult))
            put(dve.tensor_tensor(s2, b_, b_, ALU.mult))
            link(dve.tensor_scalar(one_a, na, 1.0, None, ALU.add))
            put(dve.tensor_tensor(s_, na, na, ALU.mult))
            link(dve.tensor_tensor(den, one_a, one_a, ALU.mult))
            put(dve.tensor_tensor(s_, s_, s2, ALU.add))
            link(dve.tensor_tensor(den, den, s2, ALU.add))
            put(dve.tensor_scalar(s_, s_, -1.0, 1.0, ALU.mult, ALU.add))
            link(dve.reciprocal(one_a, den))
            put(dve.tensor_tensor(low[:, 1, 0, first], s_, one_a, ALU.mult))
            link(dve.scalar_tensor_tensor(out=low[:, 1, 1, first], in0=b_, scalar=2.0, in1=one_a,
                                          op0=ALU.mult, op1=ALU.mult))

            def square(dst, z):
                put(dve.tensor_tensor(tmp_sq, z, z, ALU.mult))
                done = put(dve.scalar_tensor_tensor(out=dst[:, 1, :], in0=z[:, 0, :], scalar=2.0, in1=z[:, 1, :],
                                                    op0=ALU.mult, op1=ALU.mult))
                dve.wait_ge(chain, done - 1)
                return put(dve.tensor_tensor(dst[:, 0, :], tmp_sq[:, 0, :], tmp_sq[:, 1, :], ALU.subtract))

            def product(dst, many, one):
                m = many.shape[1]
                shape = [P, m, 2, HH]
                re = one[:, 0:1, :].rearrange("p (m r) h -> p m r h", m=1).to_broadcast(shape)
                im = one[:, 1:2, :].rearrange("p (m r) h -> p m r h", m=1).to_broadcast(shape)
                put(dve.tensor_tensor(tmp_re[:, 0:m], many, re, ALU.mult))
                link(dve.tensor_tensor(tmp_im[:, 0:m], many, im, ALU.mult))
                put(dve.tensor_tensor(dst[:, :, 0, :], tmp_re[:, 0:m, 0, :], tmp_im[:, 0:m, 1, :], ALU.subtract))
                return put(dve.tensor_tensor(dst[:, :, 1, :], tmp_re[:, 0:m, 1, :], tmp_im[:, 0:m, 0, :], ALU.add))

            there = lambda count: dve.wait_ge(chain, count)
            lw, hg, gn = (fam[:, :, :, first] for fam in (low, high, gain))
            there(square(lw[:, 2], lw[:, 1]))
            w4_at = square(lw[:, 4], lw[:, 2])
            w3_at = product(lw[:, 3:4], lw[:, 1:2], lw[:, 2])
            there(w4_at)
            w8_at = square(hg[:, 1], lw[:, 4])
            there(w3_at)
            low_at = product(lw[:, 5:8], lw[:, 1:4], lw[:, 4])
            there(w8_at)
            link(dve.tensor_scalar(hg[:, 1, 1, :], hg[:, 1, 1, :], -1.0, None, ALU.mult))
            w16_at = square(hg[:, 2], hg[:, 1])
            there(low_at)
            dve.engine_nop().then_inc(families, 1)
            put(dve.tensor_scalar(gn[:, 0, 0, :], br_p, 2.0, None, ALU.mult))
            put(dve.tensor_scalar(gn[:, 0, 1, :], bi_p, -2.0, None, ALU.mult))
            there(w16_at)
            w32_at = square(hg[:, 4], hg[:, 2])
            w24_at = product(hg[:, 3:4], hg[:, 1:2], hg[:, 2])
            there(w32_at)
            w64_at = square(w64, hg[:, 4])
            there(w24_at)
            high_at = product(hg[:, 5:8], hg[:, 1:4], hg[:, 4])
            there(w64_at)
            dve.engine_nop().then_inc(families, 1)
            w128_at = square(w128, w64)
            gain1_at = product(gn[:, 1:2], gn[:, 0:1], w64)
            there(w128_at)
            there(gain1_at)
            there(product(gn[:, 2:4], gn[:, 0:2], w128))
            dve.engine_nop().then_inc(families, 1)
            dve.wait_ge(ld_c, 16 * 3)
            dve.wait_ge(firsts, 4)
            dve.wait_ge(spread, 6)

            def group(g, half):
                if not (isinstance(g, int) and g < 2):
                    dve.wait_ge(gen_mm, g - 1)
                hs = slice(g * 2 * GH, (g + 1) * 2 * GH) if isinstance(g, int) else bass.ds(g * 2 * GH, 2 * GH)
                n = 2 * GH
                for r in range(2):
                    xs = high[:, :, r, hs].rearrange("p (m o) h -> p h m o", o=1).to_broadcast([P, n, 8, 8])
                    ys = low[:, :, r, hs].rearrange("p (o m) h -> p h o m", o=1).to_broadcast([P, n, 8, 8])
                    dve.tensor_tensor(prod[half][r].rearrange("p (h i j) -> p h i j", h=n, i=8), xs, ys,
                                      ALU.mult).then_inc(multiplied, 1)
                if isinstance(g, int) and g == 0:
                    dve.wait_ge(spread, 10)
                for r, c in enumerate((ca, cb)):
                    xs = c[:, :, hs].rearrange("p (c o) h -> p h c o", o=1).to_broadcast([P, n, CH, A_N])
                    ys = gain[:, :, r, hs].rearrange("p (o m) h -> p h o m", o=1).to_broadcast([P, n, CH, A_N])
                    dve.tensor_tensor(prod[half][2 + r].rearrange("p (h c a) -> p h c a", h=n, c=CH), xs, ys,
                                      ALU.mult).then_inc(multiplied, 1)
                dve.wait_ge(multiplied, 4 * g + 2)
                part = slice(0, GC // GH * SUMMED)
                dve.tensor_tensor(prod[half][0][:, part], prod[half][0][:, part], prod[half][1][:, part],
                                  ALU.add).then_inc(summed, 1)

            for g in range(2):
                group(g, g)
            dve.wait_ge(spread, 15)
            with dve.Fori(1, GROUPS // 2) as i:
                for half in range(2):
                    group(2 * i + half, half)
            dve.wait_ge(ld_w, 16 * 9)
            dve.wait_ge(consts, 8)

            def statistics(b, k, source, st, ag):
                if not b.real:
                    return
                settle(dve)
                dve.wait_ge(taken[source], b.n + 1)
                src = tokens_of(b)
                for t in range(TT):
                    dve.bn_stats(stats[k][:, t, :], src[:, t, :]).then_inc(st, 1)
                dve.wait_ge(st, 2 * b.n + 2)
                if not (b.static and b.n == 0):
                    dve.wait_ge([xn_done, xn2_done][k], b.n)
                dve.memset(carrier[:], 0.0)
                for t in range(TT):
                    dve.bn_aggr(mean_var[k][:, t, :], stats[k][:, t, :]).then_inc(ag, 1)

            def normalize(b, k, dst, reader, rs, done):
                if not b.real:
                    return
                src = tokens_of(b)
                if not (b.static and b.n == 0):
                    dve.wait_ge(filled[reader], b.n)
                dve.wait_ge(rs, b.n + 1)
                for t in range(TT):
                    last = dve.tensor_scalar(dst[:, t, :], src[:, t, :], mean_var[k][:, t, 0:1],
                                             rstd[k][:, t:t + 1], ALU.subtract, ALU.mult)
                last.then_inc(done, 1)

            def tokens_of(b):
                return h_all[:, b.index()].rearrange("p c t f -> p (c t) f")

            def row_max(b, u):
                if not b.real:
                    return
                g, half = u // 2, u % 2
                if u == 0 and not (b.static and b.n == 0):
                    dve.wait_ge(filled["mt"], b.n)
                for i in range(2):
                    dve.wait_ge(max_mm, NH * b.n + 2 * u + i + 1)
                    dve.tensor_reduce(neg_max[:, :, 2 * half + i, g], max_ps[:, i].rearrange("p (t k) -> p t k", t=TT),
                                      AX.X, ALU.max, negate=True).then_inc(max_red, 1)

            def take_ctx(b, half):
                if not b.real:
                    return
                dve.wait_ge(pv_mm, 4 * b.n + 2 * half + 2)
                if not (b.static and b.n == 0):
                    dve.wait_ge(filled["t4b"], b.n)
                dve.tensor_copy(ctx_raw[:, 2 * half:2 * half + 2, :].rearrange("p g t -> p (g t)"),
                                ctx_ps[:]).then_inc(ctx_out[half], 1)

            def take(name, s):
                b = s.back(-shift_of[name])
                if not b.real:
                    return
                src = misc[FILLS.index(name) % MISC]
                dve.wait_ge(filled[name], b.n + 1)
                if name in ("down", "wo"):
                    if name == "wo":
                        dve.wait_ge(bias_in, b.n + 1)
                    h = tokens_of(b)
                    dve.tensor_tensor(h, src[:].rearrange("p (t f) -> p t f", t=TT), h, ALU.add) \
                        .then_inc(taken[name], 1)
                elif name in ("t4a", "t4b"):
                    t = int(name == "t4b")
                    heads = src[:].rearrange("p (g j d) -> p g j d", g=GQ, j=NKV)
                    if not (b.static and b.n == 0):
                        dve.wait_ge(filled["t5"], b.n)
                    dve.reciprocal(ctx_sum[:, t], heads[:, :, :, HD]).then_inc(sumd, 1)
                    dve.wait_ge(sumd, 2 * b.n + t + 1)
                    inv = ctx_sum[:, t].rearrange("p g (j o) -> p g j o", o=1).to_broadcast([P, GQ, NKV, HD])
                    dve.tensor_tensor(ctx_n[:, t].rearrange("p j g d -> p g j d"), heads[:, :, :, 0:HD], inv,
                                      ALU.mult).then_inc(taken[name], 1)
                elif name in ("qkv0", "qkv1"):
                    t = int(name[-1])
                    if not (b.static and b.n == 0):
                        dve.wait_ge(rope_m, 6 * b.n)
                    if not (b.static and b.n < 2):
                        dve.wait_ge(copied[b.parity], 48 * b.half)
                    dve.tensor_tensor(qkv[:, t, 0:QK_COLS], src[:, 0:QK_COLS], bqkv_sb[:, 0:QK_COLS], ALU.add)
                    dve.tensor_tensor(v_max[b.parity][:, t, :, 0:HD],
                                      src[:, QK_COLS:QKV].rearrange("p (j d) -> p j d", j=NKV),
                                      bqkv_sb[:, QK_COLS:QKV].rearrange("p (j d) -> p j d", j=NKV),
                                      ALU.add).then_inc(taken[name], 1)
                elif name == "router":
                    dve.tensor_copy(logits[:, b.index(), :].rearrange("p c e -> p (c e)"), src[:, 0:TT * NE]) \
                        .then_inc(taken[name], 1)
                elif name == "mt":
                    if not (b.static and b.n == 0):
                        dve.wait_ge(mparted, b.n)
                    dve.tensor_copy(neg_max_t[:], src[0:NH, 0:SEQ]).then_inc(taken[name], 1)

            def square(b):
                if not b.real:
                    return
                dve.wait_ge(taken["up"], b.n + 1)
                if not (b.static and b.n == 0):
                    dve.wait_ge(filled["down"], b.n)
                dve.tensor_tensor(hid[:], hid_relu[:], hid_relu[:], ALU.mult).then_inc(squared, 1)

            def step(s):
                near, far, pre, post = s.back(-1), s.back(-2), s.back(-3), s.back(1)
                row_max(near, 2)
                take_ctx(post, 1)
                row_max(near, 3)
                take("t4a", s)
                take("t4b", s)
                row_max(near, 4)
                take("wo", s)
                statistics(post, 1, "wo", st2, ag2)
                row_max(near, 5)
                normalize(post, 1, xn2, "t6", rs2, xn2_done)
                take_ctx(s, 0)
                row_max(near, 6)
                statistics(pre, 0, "t1", st1, ag1)
                row_max(near, 7)
                normalize(pre, 0, xn, "t2", rs1, xn_done)
                take("mt", s)
                row_max(far, 0)
                square(post)
                take("down", s)
                take("router", s)
                row_max(far, 1)
                take("qkv0", s)
                take("qkv1", s)

            steps(dve, step)

            lg = logits[:].rearrange("p c (t e) -> p (c t) e", e=NE)
            per_tile = lambda m: m.rearrange("p (t o) -> p t o", o=1).to_broadcast([P, tiles, NE])
            dve.wait_ge(taken["router"], CH)
            dve.wait_ge(filled["mt"], CH)
            dve.wait_ge(filled["down"], CH)
            put(dve.memset(any_gate[:, 1:2], 1.0))
            link(dve.tensor_reduce(top1, lg, AX.X, ALU.max))
            link(dve.tensor_tensor(is_top, lg, per_tile(top1), ALU.is_equal))
            link(dve.scalar_tensor_tensor(out=others, in0=is_top, scalar=-3.0e38, in1=lg, op0=ALU.mult,
                                          op1=ALU.add))
            link(dve.tensor_reduce(top2, others, AX.X, ALU.max))
            dve.tensor_tensor(top2, top2, top1, ALU.subtract).then_inc(gaps, 1)
            link(dve.tensor_reduce(n_top, is_top, AX.X, ALU.add))
            link(dve.tensor_scalar(n_top, n_top, 1.0, None, ALU.is_equal))
            dve.wait_ge(gap_exp, 1)
            link(dve.tensor_scalar(exp_gap, exp_gap, 1.0, None, ALU.add))
            link(dve.tensor_scalar(exp_gap, exp_gap, 1.0, None, ALU.is_le))
            link(dve.tensor_tensor(gate, exp_gap, n_top, ALU.mult))
            dve.tensor_reduce(any_gate[:, 0:1], gate, AX.X, ALU.max).then_inc(gated, 1)
            link(dve.tensor_tensor(weight.rearrange("p (t e) -> p t e", e=NE), is_top, per_tile(gate), ALU.mult))
            dve.wait_ge(count_mm, 1)
            dve.tensor_copy(routed_n[:], misc[0][0:1, 0:1]).then_inc(counted, 1)
            with if_routed(dve):
                for i in range(2):
                    dve.wait_ge(stored[i], 16 * CH // 2)
                dve.memset(carrier[:], 0.0).then_inc(ex_add, 1)
                with dve.Fori(0, NE) as e:
                    with dve.Fori(0, CH) as c:
                        n = e * CH + c
                        dve.wait_ge(ex_relu, n + 1)
                        dve.tensor_tensor(hid[:], hid_relu[:], hid_relu[:], ALU.mult).then_inc(ex_hid, 1)
                        dve.wait_ge(ex_down, n + 1)
                        for t in range(TT):
                            h = h_all[:, bass.ds(c, 1), t, :].rearrange("p c f -> p (c f)")
                            ins = dve.scalar_tensor_tensor(
                                out=h, in0=misc[1][:, D * t:D * (t + 1)],
                                scalar=weight[:, bass.ds(c * (TT * NE) + e + t * NE, 1)], in1=h,
                                op0=ALU.mult, op1=ALU.add)
                        ins.then_inc(ex_add, 1)


def kernel(**inputs):
    import numpy as _np
    import concourse.bacc as _bacc
    from concourse import mybir as _mybir
    from concourse.bass_utils import run_bass_kernel_spmd as _run

    def pair_order(a):
        return a.reshape(*a.shape[:-1], 2, 128).swapaxes(-1, -2).reshape(a.shape)

    x = _np.asarray(inputs["x"])
    b_ri = _np.asarray(inputs["L0_tok_B_ri"])
    pole = _np.stack([pair_order(_np.asarray(a).T).reshape(64, 2, 128).swapaxes(0, 1).reshape(128, 128)
                      for a in (inputs["L0_tok_inv_A_real"], inputs["L0_tok_A_imag"], b_ri[..., 0], b_ri[..., 1])],
                     axis=1)
    arrays = {
        "xh": pair_order(x.transpose(3, 2, 0, 1)),
        "log_dt": pair_order(_np.asarray(inputs["L0_tok_log_dt"])).reshape(2, 128),
        "pole": pole,
        "wqkv": _np.concatenate([_np.asarray(inputs[f"L0_attn_W{k}"]) for k in "qkv"]).T,
        "bqkv": _np.concatenate([_np.asarray(inputs[f"L0_attn_b{k}"]) for k in "qkv"])[None, :],
        "wo": _np.asarray(inputs["L0_attn_Wo"]).T,
        "bo": _np.asarray(inputs["L0_attn_bo"])[None, :],
        "ws1": _np.asarray(inputs["L0_ffn_Ws1"]),
        "ws2": _np.asarray(inputs["L0_ffn_Ws2"]),
        "w1": _np.asarray(inputs["L0_ffn_W1"]),
        "w2": _np.asarray(inputs["L0_ffn_W2"]),
        "wr": _np.asarray(inputs["L0_ffn_Wr"]),
    }
    f32 = _np.float32
    inv_freq = (f32(1.0) / f32(10000.0) ** (_np.arange(0, HD, 2, dtype=f32) / f32(HD))).astype(f32)
    angle = _np.arange(SEQ, dtype=f32)[:, None] * inv_freq[None, :]
    arrays["cos_t"] = _np.concatenate([_np.cos(angle)] * 2, -1).astype(f32)
    arrays["sin_t"] = _np.concatenate([-_np.sin(angle), _np.sin(angle)], -1).astype(f32)
    arrays["ident"] = _np.eye(128, dtype=f32)

    nc = _bacc.Bacc("TRN2", target_bir_lowering=False, num_devices=1)
    names, args = {}, []
    for name, a in arrays.items():
        a = _np.ascontiguousarray(a)
        names[f"in_{name}"] = a
        args.append(nc.dram_tensor(f"in_{name}", a.shape, _mybir.dt.from_np(a.dtype), kind="ExternalInput").ap())
    out = nc.dram_tensor("out_0", (CH, SEQ, D), _mybir.dt.float32, kind="ExternalOutput").ap()
    vit_block_kernel(nc, *args, out)
    r = _run(nc, [names], core_ids=[0])
    return r.results[0]["out_0"]
```
